# Optimizing a Trainium2 kernel written in Bass

```python
import numpy as np
import jax
import jax.numpy as jnp

def _softmax(x, axis=-1):
    return jax.nn.softmax(x, axis=axis)

def _gelu(x):
    return jax.nn.gelu(x, approximate=True)

def _silu(x):
    return jax.nn.silu(x)

def _sigmoid(x):
    return jax.nn.sigmoid(x)

def _layernorm(x, axis=-1, eps=1e-05):
    m = jnp.mean(x, axis=axis, keepdims=True)
    v = jnp.var(x, axis=axis, keepdims=True)
    return (x - m) / jnp.sqrt(v + eps)

def _scatter_add(tgt, idx, src, axis=0):
    return tgt.at[idx].add(src)

def _segment_sum(src, seg, n):
    return jax.ops.segment_sum(src, seg, n)
kernel_name = 'mk_flamingo_gated_d1_seqx_r4_ed6da2'

def setup_inputs(seed: int=0):
    np.random.seed(seed)
    _w = jnp.asarray

    def _rec_inputs():
        import jax
        import jax.numpy as jnp
        _rk = jax.random.key(seed)
        x = -0.0003929 + 0.9999 * jax.random.normal(jax.random.fold_in(_rk, 1), (8, 512, 512), jnp.float32)
        _lenS = 512 - jax.random.randint(jax.random.fold_in(_rk, 7), (8,), 0, max(1, 512 // 4) + 1, jnp.int32)
        _lenS2 = 1601 - jax.random.randint(jax.random.fold_in(_rk, 8), (8,), 0, max(1, 1601 // 4) + 1, jnp.int32)
        _ctx_2048P = jax.random.normal(jax.random.fold_in(_rk, 11), (8, 16, 512), jnp.float32)
        _ctx_2048c = jax.random.dirichlet(jax.random.fold_in(_rk, 511), 0.3 * jnp.ones((16,), jnp.float32), (8, 1601))
        _ctx_2048t = jnp.einsum('bsk,bkd->bsd', _ctx_2048c, _ctx_2048P)
        _ctx_2048t = _ctx_2048t * jax.lax.rsqrt(jnp.mean(jnp.square(_ctx_2048t)) + 1e-12) * 0.953939
        ctx_2048 = -0.000514642 + 1.00011 * (_ctx_2048t + 0.3 * jax.random.normal(jax.random.fold_in(_rk, 611), (8, 1601, 512), jnp.float32))
        _g = jax.random.normal(jax.random.fold_in(_rk, 9001), (2, 1), jnp.float32)
        _g = jnp.sign(_g) * jnp.maximum(jnp.abs(_g), 1.0) + (_g == 0) * 1.0
        g_xattn = _g[0]
        g_ffn = _g[1]
        return (x, ctx_2048, g_xattn, g_ffn)
    x, ctx_2048, g_xattn, g_ffn = _rec_inputs()

    def _L0_xattn_setup():
        import jax, jax.numpy as jnp
        import numpy as np
        NUM_HEADS = 16

        def _qdq(x):
            s = jnp.maximum(jnp.max(jnp.abs(x), axis=-1, keepdims=True) / 127.0, 1e-08)
            return jnp.clip(jnp.round(x / s), -127.0, 127.0) * s
        key = jax.random.key(seed)
        ks = jax.random.split(key, 8)
        B, N, M, D = (2, 1024, 128, 512)
        w_std = 0.02
        return {'x': jax.random.normal(ks[0], (B, N, D), jnp.float32), 'cond': jax.random.normal(ks[1], (B, M, D), jnp.float32), 'wq': jax.random.normal(ks[2], (D, D), jnp.float32) * w_std, 'bq': jax.random.normal(ks[3], (D,), jnp.float32) * w_std, 'wkv': jax.random.normal(ks[4], (2 * D, D), jnp.float32) * w_std, 'bkv': jax.random.normal(ks[5], (2 * D,), jnp.float32) * w_std, 'wp': jax.random.normal(ks[6], (D, D), jnp.float32) * w_std, 'bp': jax.random.normal(ks[7], (D,), jnp.float32) * w_std}
    _L0_xattn_all = _L0_xattn_setup()
    _L0_xattn_in = {k: v for k, v in _L0_xattn_all.items() if k in ('wq', 'bq', 'wkv', 'bkv', 'wp', 'bp')}
    del _L0_xattn_all

    def _L0_ffn_setup():
        import jax, jax.numpy as jnp
        import numpy as np
        E = 32
        K = 4
        G = 4
        TG = 2
        H = 512
        F = 256
        FS = 512
        SCALE = 2.0
        B, S = (2, 256)
        N = B * S
        CAP = 2 * (N * K // E)

        def _gate(x, gate_w, gate_bias):
            logits = x @ gate_w.T
            scores = jax.nn.sigmoid(logits)
            sc = scores + gate_bias
            n = x.shape[0]
            grp = sc.reshape(n, G, E // G)
            group_scores = jax.lax.top_k(grp, 2)[0].sum(-1)
            _, gidx = jax.lax.top_k(group_scores, TG)
            gmask = jnp.zeros((n, G), sc.dtype).at[jnp.arange(n)[:, None], gidx].set(1.0)
            smask = jnp.repeat(gmask, E // G, axis=1)
            tmp = jnp.where(smask > 0, sc, 0.0)
            _, topk_idx = jax.lax.top_k(tmp, K)
            topk_w = jnp.take_along_axis(scores, topk_idx, axis=1)
            topk_w = topk_w / (topk_w.sum(-1, keepdims=True) + 1e-20)
            return (topk_idx, topk_w * SCALE)

        def _moe(x, topk_idx, topk_w, w1, w2, w3):
            n = x.shape[0]
            flat_e = topk_idx.reshape(-1)
            oh = jax.nn.one_hot(flat_e, E, dtype=jnp.int32)
            pos = (jnp.cumsum(oh, axis=0) * oh).sum(-1) - 1
            keep = pos < CAP
            slot = jnp.where(keep, pos, CAP)
            x_rep = jnp.repeat(x, K, axis=0)
            buf = jnp.zeros((E, CAP, H), x.dtype).at[flat_e, slot].set(x_rep, mode='drop')
            h = jax.nn.silu(jnp.einsum('ech,ehf->ecf', buf, w1)) * jnp.einsum('ech,ehf->ecf', buf, w3)
            ob = jnp.einsum('ecf,efh->ech', h, w2)
            y = ob[flat_e, jnp.minimum(slot, CAP - 1)]
            y = jnp.where(keep[:, None], y, 0.0)
            return (y.reshape(n, K, H) * topk_w[:, :, None]).sum(1)
        key = jax.random.key(seed)
        ks = jax.random.split(key, 9)
        w = 0.02
        return {'hidden_states': jax.random.normal(ks[0], (B, S, H), jnp.float32), 'gate_w': jax.random.normal(ks[1], (E, H), jnp.float32) * w, 'gate_bias': jax.random.normal(ks[2], (E,), jnp.float32) * w, 'w1': jax.random.normal(ks[3], (E, H, F), jnp.float32) * w, 'w2': jax.random.normal(ks[4], (E, F, H), jnp.float32) * w, 'w3': jax.random.normal(ks[5], (E, H, F), jnp.float32) * w, 'shared_gate': jax.random.normal(ks[6], (H, FS), jnp.float32) * w, 'shared_up': jax.random.normal(ks[7], (H, FS), jnp.float32) * w, 'shared_down': jax.random.normal(ks[8], (FS, H), jnp.float32) * w}
    _L0_ffn_all = _L0_ffn_setup()
    _L0_ffn_in = {k: v for k, v in _L0_ffn_all.items() if k in ('gate_w', 'gate_bias', 'w1', 'w2', 'w3', 'shared_gate', 'shared_up', 'shared_down')}
    del _L0_ffn_all
    return {'x': x, 'ctx_2048': ctx_2048, 'g_xattn': g_xattn, 'g_ffn': g_ffn, 'L0_xattn_wq': _L0_xattn_in['wq'], 'L0_xattn_bq': _L0_xattn_in['bq'], 'L0_xattn_wkv': _L0_xattn_in['wkv'], 'L0_xattn_bkv': _L0_xattn_in['bkv'], 'L0_xattn_wp': _L0_xattn_in['wp'], 'L0_xattn_bp': _L0_xattn_in['bp'], 'L0_ffn_gate_w': _L0_ffn_in['gate_w'], 'L0_ffn_gate_bias': _L0_ffn_in['gate_bias'], 'L0_ffn_w1': _L0_ffn_in['w1'], 'L0_ffn_w2': _L0_ffn_in['w2'], 'L0_ffn_w3': _L0_ffn_in['w3'], 'L0_ffn_shared_gate': _L0_ffn_in['shared_gate'], 'L0_ffn_shared_up': _L0_ffn_in['shared_up'], 'L0_ffn_shared_down': _L0_ffn_in['shared_down']}

def reference(x, ctx_2048, g_xattn, g_ffn, L0_xattn_wq, L0_xattn_bq, L0_xattn_wkv, L0_xattn_bkv, L0_xattn_wp, L0_xattn_bp, L0_ffn_gate_w, L0_ffn_gate_bias, L0_ffn_w1, L0_ffn_w2, L0_ffn_w3, L0_ffn_shared_gate, L0_ffn_shared_up, L0_ffn_shared_down):
    import jax
    import jax.numpy as jnp

    def _L0_xattn_ref(x, cond, wq, bq, wkv, bkv, wp, bp):
        import jax, jax.numpy as jnp
        import numpy as np
        NUM_HEADS = 16

        def _qdq(x):
            s = jnp.maximum(jnp.max(jnp.abs(x), axis=-1, keepdims=True) / 127.0, 1e-08)
            return jnp.clip(jnp.round(x / s), -127.0, 127.0) * s
        B, N, C = x.shape
        M = cond.shape[1]
        H = NUM_HEADS
        Dh = C // H
        q = _qdq(x) @ _qdq(wq).T + bq
        kv = cond @ wkv.T + bkv
        k, v = jnp.split(kv, 2, axis=-1)
        q = q.reshape(B, N, H, Dh)
        k = k.reshape(B, M, H, Dh)
        v = v.reshape(B, M, H, Dh)
        scale = 1.0 / np.sqrt(Dh)
        attn = jax.nn.softmax(jnp.einsum('bnhd,bmhd->bhnm', q, k) * scale, axis=-1)
        o = jnp.einsum('bhnm,bmhd->bnhd', attn, v).reshape(B, N, C)
        out = _qdq(o) @ _qdq(wp).T + bp
        return out

    def _L0_ffn_ref(hidden_states, gate_w, gate_bias, w1, w2, w3, shared_gate, shared_up, shared_down):
        import jax, jax.numpy as jnp
        import numpy as np
        E = 32
        K = 4
        G = 4
        TG = 2
        H = 512
        F = 256
        FS = 512
        SCALE = 2.0
        B, S = (2, 256)
        N = B * S
        CAP = 2 * (N * K // E)

        def _gate(x, gate_w, gate_bias):
            logits = x @ gate_w.T
            scores = jax.nn.sigmoid(logits)
            sc = scores + gate_bias
            n = x.shape[0]
            grp = sc.reshape(n, G, E // G)
            group_scores = jax.lax.top_k(grp, 2)[0].sum(-1)
            _, gidx = jax.lax.top_k(group_scores, TG)
            gmask = jnp.zeros((n, G), sc.dtype).at[jnp.arange(n)[:, None], gidx].set(1.0)
            smask = jnp.repeat(gmask, E // G, axis=1)
            tmp = jnp.where(smask > 0, sc, 0.0)
            _, topk_idx = jax.lax.top_k(tmp, K)
            topk_w = jnp.take_along_axis(scores, topk_idx, axis=1)
            topk_w = topk_w / (topk_w.sum(-1, keepdims=True) + 1e-20)
            return (topk_idx, topk_w * SCALE)

        def _moe(x, topk_idx, topk_w, w1, w2, w3):
            n = x.shape[0]
            flat_e = topk_idx.reshape(-1)
            oh = jax.nn.one_hot(flat_e, E, dtype=jnp.int32)
            pos = (jnp.cumsum(oh, axis=0) * oh).sum(-1) - 1
            keep = pos < CAP
            slot = jnp.where(keep, pos, CAP)
            x_rep = jnp.repeat(x, K, axis=0)
            buf = jnp.zeros((E, CAP, H), x.dtype).at[flat_e, slot].set(x_rep, mode='drop')
            h = jax.nn.silu(jnp.einsum('ech,ehf->ecf', buf, w1)) * jnp.einsum('ech,ehf->ecf', buf, w3)
            ob = jnp.einsum('ecf,efh->ech', h, w2)
            y = ob[flat_e, jnp.minimum(slot, CAP - 1)]
            y = jnp.where(keep[:, None], y, 0.0)
            return (y.reshape(n, K, H) * topk_w[:, :, None]).sum(1)
        b, s, h = hidden_states.shape
        x = hidden_states.reshape(-1, h)
        topk_idx, topk_w = _gate(x, gate_w, gate_bias)
        out = _moe(x, topk_idx, topk_w, w1, w2, w3)
        shared = jax.nn.silu(x @ shared_gate) * (x @ shared_up) @ shared_down
        return (out + shared).reshape(b, s, h)
    x = x + jnp.tanh(g_xattn[0]) * _L0_xattn_ref(_layernorm(x, axis=-1), ctx_2048, L0_xattn_wq, L0_xattn_bq, L0_xattn_wkv, L0_xattn_bkv, L0_xattn_wp, L0_xattn_bp)
    x = x + jnp.tanh(g_ffn[0]) * _L0_ffn_ref(_layernorm(x, axis=-1), L0_ffn_gate_w, L0_ffn_gate_bias, L0_ffn_w1, L0_ffn_w2, L0_ffn_w3, L0_ffn_shared_gate, L0_ffn_shared_up, L0_ffn_shared_down)
    return x

_drawn_inputs = setup_inputs


def setup_inputs(seed=0):
    import zlib

    import numpy as np

    out = dict(_drawn_inputs(seed))
    spreads = {}
    factors = {'L0_xattn_wq': 8.0,
     'L0_xattn_bq': 8.0,
     'L0_xattn_bkv': 7.56,
     'L0_xattn_bp': 3.667,
     'L0_ffn_gate_w': 3.656,
     'L0_ffn_gate_bias': 6.096,
     'L0_ffn_w1': 3.494,
     'L0_ffn_w2': 3.427,
     'L0_ffn_w3': 3.433}
    for name, (base, spread) in spreads.items():
        noise = np.random.default_rng([zlib.crc32(name.encode()), seed]).standard_normal(out[name].shape)
        drawn = base * np.exp(spread * noise) if base else spread * noise
        out[name] = jnp.asarray(drawn.astype(out[name].dtype))
    for name, factor in factors.items():
        out[name] = (out[name] * factor).astype(out[name].dtype)
    return out
```

```python
from contextlib import ExitStack

import concourse.bass as bass
from concourse import mybir

FP32, FP16, BF16, I32, U32 = (mybir.dt.float32, mybir.dt.float16, mybir.dt.bfloat16,
                              mybir.dt.int32, mybir.dt.uint32)
ALU = mybir.AluOpType
ACT = mybir.ActivationFunctionType
X_AXIS = mybir.AxisListType.X

B, N, D = 8, 512, 512
M = 1601
HEADS, DH = 16, 32
P = 128
TT = N // P
DC = D // P
KT = (M + P - 1) // P
GROUPS, GH = 4, 4
PIECES = 4
PIECE = [M // PIECES + (1 if i < M % PIECES else 0) for i in range(PIECES)]
PIECE_AT = [sum(PIECE[:i]) for i in range(PIECES)]
E, TOPK, EGROUPS, EPG, CAP, F, FS = 32, 4, 4, 8, 128, 256, 512
TOK = B * N
FSC, FC = FS // P, F // P
KSPLIT = 3 * DH
SCALE = 1.0 / float(DH) ** 0.5
EPS = 1e-5
ROUND = 12582912.0
CT_SLOTS = 3
DMA = 16


def rows(t):
    return min(P, M - t * P)


def prep_tiles(g, step=None):
    score_max = [("max", g, j, qt, i) for j in range(GH) for qt in range(TT) for i in range(PIECES)]
    at = [[] for _ in range(KT)]
    at[0] = [("q", g), ("k", g, 0)]
    for i in range(1, PIECES):
        at[i] = [("k", g, i)]
    first, last = PIECES + 1, KT - 1
    per = -(-len(score_max) // (last - first))
    for s in range(first, last):
        at[s] = score_max[(s - first) * per:(s - first + 1) * per]
    at[last] = [("maxT", g)]
    return at[step] if step is not None else [t for s in at for t in s]


def setup_order():
    return ([("wqT", c) for c in range(DC)] + [("wpT", c) for c in range(DC)]
            + [("wkT", c) for c in range(DC)] + [("wvT", c) for c in range(DC)]
            + [("gateT",), ("swp",)])


def batch_order():
    order = [("xT", c) for c in range(DC)] + [("sx",)]
    for t in range(KT):
        order.append(("ctxT", t))
        if t:
            order.append(("v", t - 1))
    order.append(("v", KT - 1))
    order += prep_tiles(0)
    for g in range(GROUPS):
        for kt in range(KT):
            if g + 1 < GROUPS:
                order += prep_tiles(g + 1, kt)
            if kt == 1 and g:
                order += [("oT", g - 1), ("sumT", g - 1)]
    order += [("oT", GROUPS - 1), ("sumT", GROUPS - 1)]
    order += [("oiT", c) for c in range(DC)] + [("y", t) for t in range(TT)]
    order += [("hT", c) for c in range(DC)] + [("logits",)]
    for f in range(FSC):
        order += [("gate", f), ("up", f)]
    order += [("cum",), ("total",)]
    order += [("down", t) for t in range(TT)]
    if len(order) % 2:
        order.append(("even",))
    return order


def expert_order():
    order = []
    for u in range(2):
        order += [("hgT", u), ("eg", u), ("eu", u), ("ey", u)]
    return order


class Ring:

    def __init__(self):
        self.n, self.base, self.per, at = {}, {}, {}, 0
        for stage, order, times in (("setup", setup_order(), 1), ("batch", batch_order(), B),
                                    ("expert", expert_order(), E // 2)):
            assert len(order) % 2 == 0 and len(set(order)) == len(order)
            for i, key in enumerate(order):
                self.n[(stage,) + key] = i
            self.base[stage], self.per[stage] = at // 2, len(order) // 2
            at += len(order) * times

    def bank(self, *key):
        return self.n[key] % 2

    def done(self, it, *key):
        stage = key[0]
        k = self.base[stage] + self.n[key] // 2 + 1
        return k if stage == "setup" else it * self.per[stage] + k


class Steps:

    def __init__(self, engine, sem, wait_carrier=None):
        self.engine, self.sem, self.wait_carrier = engine, sem, wait_carrier
        self.base, self.k, self.it, self.per = 0, 0, None, 0

    def mark(self, instruction):
        self.k += 1
        instruction.then_inc(self.sem, 1)

    def value(self):
        return self.base + self.k if self.it is None else self.it * self.per + (self.base + self.k)

    def settle(self):
        self.engine.wait_ge(self.sem, self.value())

    def carry_wait(self):
        self.engine.sem_inc(self.wait_carrier, 1)

    def enter(self, it, per):
        self.base, self.k, self.it, self.per = self.base + self.k, 0, it, per

    def leave(self, times):
        assert self.k <= self.per, (self.k, self.per)
        self.settle()
        if self.k < self.per:
            self.engine.sem_inc(self.sem, self.per - self.k)
        self.base, self.k, self.it = self.base + self.per * times, 0, None


def build(nc, x, ctx_in, g_xattn, g_ffn, wq, bq, wkv, bkv, wp, bp, gate_w, gate_bias, w1, w2, w3,
          shared_gate, shared_up, shared_down, out):
    x_v = x.rearrange("b (t p) d -> b p t d", p=P)
    out_v = out[0:TOK, :].rearrange("(b t p) d -> b p t d", p=P, t=TT)
    h_scr = nc.dram_tensor("h_rows", [TOK + CAP, D], FP32).ap()
    h_v = h_scr[0:TOK, :].rearrange("(b t p) d -> b p t d", p=P, t=TT)
    slot_scr = nc.dram_tensor("slot_rows", [E * CAP, 2], FP32).ap()
    slot_v = slot_scr.rearrange("(e c) w -> e c w", c=CAP)
    w1_v = w1.rearrange("e (c p) f -> e p c f", p=P)
    w3_v = w3.rearrange("e (c p) f -> e p c f", p=P)
    w2_v = w2.rearrange("e (c p) d -> e p c d", p=P)
    max_scr = nc.dram_tensor("max_rows", [2, GH * TT, P], FP16).ap()
    ring = Ring()

    ctx = ExitStack()
    with ctx:
        def sb(name, shape, dt):
            return ctx.enter_context(nc.sbuf_tensor(name, shape, dt))

        def sem(name):
            return ctx.enter_context(nc.semaphore(name))

        ident = sb("ident", [P, P], FP32)
        identb = sb("identb", [P, P], BF16)
        tri = sb("tri", [P, P], BF16)
        onesb = sb("onesb", [P, P], BF16)
        ones = sb("ones", [P, DH], FP32)
        lane = sb("lane", [P, E], FP32)
        eps = sb("eps", [P, 1], FP32)
        wqT = sb("wqT", [P, DC, D], BF16)
        wpT = sb("wpT", [P, DC, D], BF16)
        wkv_hi = sb("wkv_hi", [P, 2, DC, D], FP16)
        wkv_lo = sb("wkv_lo", [P, 2, DC, D], FP16)
        sg = sb("sg", [P, DC, FS], FP32)
        su = sb("su", [P, DC, FS], FP32)
        sd = sb("sd", [P, FSC, D], FP32)
        gateT = sb("gateT", [P, DC, E], FP32)
        gbias = sb("gbias", [P, E], FP32)
        swq = sb("swq", [P, 4], FP32)
        swp = sb("swp", [P, 4], FP32)
        swp_row = sb("swp_row", [P, D], FP32)
        bp_row = sb("bp_row", [P, D], FP32)
        bv_row = sb("bv_row", [P, D], FP32)
        bq_col = sb("bq_col", [P, 4], FP32)
        bk_col = sb("bk_col", [P, 4], FP32)
        tanhs = sb("tanhs", [P, 2], FP32)
        xin = sb("xin", [P, TT, D], FP32)
        work = sb("work", [P, TT, D], FP32)
        q_int = sb("q_int", [P, TT, D], BF16)
        qT_int = sb("qT_int", [P, DC, N], BF16)
        stats = sb("stats", [P, TT, 6], FP32)
        mv = sb("mv", [P, TT, 2], FP32)
        std = sb("std", [P, TT], FP32)
        rstd = sb("rstd", [P, TT], FP32)
        amax = sb("amax", [P, TT], FP32)
        sx = sb("sx", [P, TT], FP32)
        inv = sb("inv", [P, TT], FP32)
        so = sb("so", [P, TT], FP32)
        sx_row = sb("sx_row", [P, N], FP32)
        ctx_raw = sb("ctx_raw", [P, CT_SLOTS, D], FP32)
        ctx_hi = sb("ctx_hi", [P, DC, M], FP16)
        ctx_lo = sb("ctx_lo", [P, DC, M], FP16)
        v_sb = sb("v_sb", [P, KT, D], FP32)
        qf = sb("qf", [P, N], FP32)
        zero_rows = qf
        q_hi = sb("q_hi", [P, N], FP16)
        q_lo = sb("q_lo", [P, N], FP16)
        k_hi = sb("k_hi", [P, M], FP16)
        k_lo = sb("k_lo", [P, M], FP16)
        k_stack = sb("k_stack", [KSPLIT + 1, 2, GH, M], FP16)
        q_stack = sb("q_stack", [KSPLIT + 1, 2, GH, N], FP16)
        piece_max = sb("piece_max", [P, GH * TT, PIECES], FP32)
        row_max = sb("row_max", [P, GH * TT], FP32)
        max_row = sb("max_row", [GH * TT, P], FP16)
        probs = sb("probs", [P, 2, GH, N], FP32)
        oT_sb = sb("oT_sb", [P, N], FP32)
        sum_sb = sb("sum_sb", [P, N], FP32)
        gate_raw = sum_sb[0:E, :]
        rsum = sb("rsum", [P, TT, GH], FP32)
        hT, actT = probs[:, 0], probs[:, 1]
        sig, gsil = oT_sb, sum_sb
        onehot = v_sb[:, 8, :].rearrange("p (t k e) -> p t k e", t=TT, k=TOPK)
        picked = v_sb[:, 9, :].rearrange("p (t k e) -> p t k e", t=TT, k=TOPK)
        scores, biased, masked, cum = (v_sb[:, 10, i * TT * E:(i + 1) * TT * E].rearrange("p (t e) -> p t e", t=TT)
                                       for i in range(4))
        top8 = v_sb[:, 11, 0:TT * E].rearrange("p (t q e) -> p t q e", t=TT, q=EGROUPS)
        gsum = sb("gsum", [P, TT, 8], FP32)
        gtop = sb("gtop", [P, TT, 8], FP32)
        gidx = sb("gidx", [P, TT, 8], U32)
        gidxf = sb("gidxf", [P, TT, 2], FP32)
        geq = sb("geq", [P, TT, 2, EGROUPS], FP32)
        gmask = sb("gmask", [P, TT, EGROUPS], FP32)
        etop = sb("etop", [P, TT, 8], FP32)
        eidx = sb("eidx", [P, TT, 8], U32)
        eidxf = sb("eidxf", [P, TT, TOPK], FP32)
        chosen = sb("chosen", [P, TT, E], BF16)
        carry = sb("carry", [P, E], FP32)
        pos = sb("pos", [P, TT, TOPK], FP32)
        over = sb("over", [P, TT, TOPK], FP32)
        slotf = sb("slotf", [P, TT, TOPK], FP32)
        slot = sb("slot", [P, TT, TOPK], I32)
        wk = sb("wk", [P, TT, TOPK], FP32)
        wsum = sb("wsum", [P, TT], FP32)
        wrec = sb("wrec", [P, TT], FP32)
        payload = sb("payload", [P, TT, TOPK, 2], FP32)
        slot_init = sb("slot_init", [P, E, 2], FP32)
        payload_i = payload[:, :, :, :].bitcast(I32)
        token = sb("token", [P, TT, TOPK], FP32)
        def part(buf, first, count, pattern, **sizes):
            return buf[:, first:first + count, :].rearrange(pattern, **sizes)

        e_w1 = part(v_sb, 0, 4, "p a (b f) -> p a b f", f=F).rearrange("p (u a) b f -> p u (a b) f", u=2)
        e_w3 = part(v_sb, 4, 4, "p a (b f) -> p a b f", f=F).rearrange("p (u a) b f -> p u (a b) f", u=2)
        e_w2 = part(v_sb, 8, 4, "p (u f) d -> p u f d", u=2)
        p_sb = probs[:, :, :, :].rearrange("p a b n -> p (a b) n")
        e_rows = [p_sb[:, u, :] for u in range(2)]
        e_rowsT = part(p_sb, 2, 2, "p u (c n) -> p u c n", c=DC)
        e_y = [p_sb[:, 4 + u, :] for u in range(2)]
        e_act = p_sb[:, 6, :].rearrange("p (u f n) -> p u f n", u=2, f=FC)
        e_sig, e_gsil = p_sb[:, 7, 0:FC * P], p_sb[:, 7, FC * P:2 * FC * P]
        e_slots = [sb(f"e_slots{u}", [P, 2], FP32) for u in range(2)]

        s_ps = [ctx.enter_context(nc.psum_tensor(f"s_ps{j}", [P, 512], FP32)) for j in range(GH)]
        r_ps = [ctx.enter_context(nc.psum_tensor(f"r_ps{i}", [P, 512], FP32)) for i in range(2)]
        o_ps = ctx.enter_context(nc.psum_tensor("o_ps", [P, 512], FP32))
        sum_ps = ctx.enter_context(nc.psum_tensor("sum_ps", [P, 512], FP32))

        consts_ready = sem("consts_ready")
        small_in = sem("small_in")
        raw_w_in = [sem(f"raw_w_in{i}") for i in range(2)]
        shared_in = sem("shared_in")
        w_int_ready = sem("w_int_ready")
        rows_init = sem("rows_init")
        row_consts_ready = sem("row_consts_ready")
        bank_full = [sem(f"bank_full{i}") for i in range(2)]
        bank_free = [sem(f"bank_free{i}") for i in range(2)]
        dve_step = sem("dve_step")
        act_step = sem("act_step")
        pool_step = sem("pool_step")
        dve_wait_carrier = sem("dve_wait_carrier")
        pool_wait_carrier = sem("pool_wait_carrier")
        tanh_ready = sem("tanh_ready")
        hi_ready = sem("hi_ready")
        x_in = sem("x_in")
        x_free = sem("x_free")
        ctx_raw_in = [sem(f"ctx_raw_in{i}") for i in range(CT_SLOTS)]
        var_ready = sem("var_ready")
        std_ready = sem("std_ready")
        q_int_ready = sem("q_int_ready")
        ctx_lo_ready = sem("ctx_lo_ready")
        v_ready = sem("v_ready")
        x_biased = sem("x_biased")
        q_split = sem("q_split")
        k_split = sem("k_split")
        stack_in = sem("stack_in")
        row_max_ready = sem("row_max_ready")
        max_row_ready = sem("max_row_ready")
        max_out = sem("max_out")
        max_in = sem("max_in")
        scores_ready = sem("scores_ready")
        probs_ready = sem("probs_ready")
        probs_used = sem("probs_used")
        heads_copied = sem("heads_copied")
        rsum_ready = sem("rsum_ready")
        o_scaled = sem("o_scaled")
        evac_act = sem("evac_act")
        h_ready = sem("h_ready")
        h_out = sem("h_out")
        scores_sig = sem("scores_sig")
        sig_ready = sem("sig_ready")
        chosen_ready = sem("chosen_ready")
        act_ready = sem("act_ready")
        out_ready = sem("out_ready")
        out_written = sem("out_written")
        route_ready = sem("route_ready")
        slots_written = sem("slots_written")
        payload_free = sem("payload_free")
        e_w_in = [sem(f"e_w_in{u}") for u in range(2)]
        e_slots_in = [sem(f"e_slots_in{u}") for u in range(2)]
        e_rows_in = [sem(f"e_rows_in{u}") for u in range(2)]
        e_sig_ready = sem("e_sig_ready")
        e_act_ready = sem("e_act_ready")
        e_y_ready = sem("e_y_ready")
        rows_added = sem("rows_added")
        experts_done = sem("experts_done")

        block = ctx.enter_context(nc.Block())

        def full(eng, it, *key):
            k = ring.bank(*key)
            eng.wait_ge(bank_full[k], ring.done(it, *key))
            return r_ps[k]

        def free_of(*key):
            return bank_free[ring.bank(*key)]

        @block.sync
        def _(sp):
            w_v = {"wq": wq.rearrange("(r p) d -> p r d", p=P), "wp": wp.rearrange("(r p) d -> p r d", p=P),
                   "wk": wkv[0:D, :].rearrange("(r p) d -> p r d", p=P),
                   "wv": wkv[D:2 * D, :].rearrange("(r p) d -> p r d", p=P)}
            sp.dma_start(probs[:, 0], w_v["wq"]).then_inc(raw_w_in[0], DMA)
            sp.dma_start(probs[:, 1], w_v["wp"]).then_inc(raw_w_in[1], DMA)
            for dst, src in ((bq_col, bq), (bk_col, bkv[0:D])):
                sp.dma_start(dst[:, :], src.rearrange("(r p) -> p r", p=P), allow_slow_non_contiguous=True).then_inc(small_in, DMA)
            for dst, src in ((bp_row, bp), (bv_row, bkv[D:2 * D]), (gbias, gate_bias)):
                sp.dma_start(dst[:, :], src.rearrange("(o n) -> o n", o=1).to_broadcast([P, src.shape[0]])
                             ).then_inc(small_in, DMA)
            for i, g_ in enumerate((g_xattn, g_ffn)):
                sp.dma_start(tanhs[:, i:i + 1], g_.rearrange("(o n) -> o n", o=1).to_broadcast([P, 1])
                             ).then_inc(small_in, DMA)
            sp.dma_start(gate_raw[:, :], gate_w).then_inc(small_in, DMA)
            sp.wait_ge(w_int_ready, 1)
            sp.dma_start(probs[:, 0], w_v["wk"]).then_inc(raw_w_in[0], DMA)
            sp.wait_ge(w_int_ready, 2)
            sp.dma_start(probs[:, 1], w_v["wv"]).then_inc(raw_w_in[1], DMA)
            sp.dma_start(sg[:, :, :], shared_gate.rearrange("(c p) n -> p c n", p=P)).then_inc(shared_in, DMA)
            sp.dma_start(su[:, :, :], shared_up.rearrange("(c p) n -> p c n", p=P)).then_inc(shared_in, DMA)
            sp.dma_start(sd[:, :, :], shared_down.rearrange("(c p) n -> p c n", p=P)).then_inc(shared_in, DMA)
            sp.wait_ge(consts_ready, 1)
            sp.dma_start(out[TOK:TOK + CAP, :], zero_rows[:, :]).then_inc(rows_init, DMA)
            sp.dma_start(h_scr[TOK:TOK + CAP, :], zero_rows[:, :]).then_inc(rows_init, DMA)
            sp.dma_start(slot_v.rearrange("e c w -> c e w"), slot_init[:, :, :]).then_inc(rows_init, DMA)
            with sp.Fori(0, B) as b:
                sp.wait_ge(x_free, b + 1)
                sp.dma_start(xin[:, :, :], x_v[b]).then_inc(x_in, DMA)
                for t in range(KT):
                    if t < CT_SLOTS:
                        sp.wait_ge(bank_full[ring.bank("batch", "ctxT", 0)], b * ring.per["batch"] + ring.base["batch"])
                    else:
                        key = ("batch", "ctxT", t - CT_SLOTS)
                        sp.wait_ge(bank_full[ring.bank(*key)], ring.done(b, *key))
                    sp.dma_start(ctx_raw[0:rows(t), t % CT_SLOTS, :],
                                 ctx_in.rearrange("b m d -> b m d")[b, t * P:t * P + rows(t), :]
                                 ).then_inc(ctx_raw_in[t % CT_SLOTS], DMA)
                for g in range(GROUPS):
                    r = g % 2
                    sp.wait_ge(q_split, b * GROUPS + g + 1)
                    for j in range(GH):
                        src = slice(j * DH, (j + 1) * DH)
                        for k, part in enumerate((q_hi, q_hi, q_lo)):
                            sp.dma_start(q_stack[k * DH:(k + 1) * DH, r, j, :], part[src, :]).then_inc(stack_in, DMA)
                    sp.wait_ge(k_split, b * GROUPS + g + 1)
                    for j in range(GH):
                        src = slice(j * DH, (j + 1) * DH)
                        for k, part in enumerate((k_hi, k_lo, k_hi)):
                            sp.dma_start(k_stack[k * DH:(k + 1) * DH, r, j, :], part[src, :]).then_inc(stack_in, DMA)
                    sp.wait_ge(max_row_ready, b * GROUPS + g + 1)
                    sp.dma_start(max_scr[r], max_row[:, :]).then_inc(max_out, DMA)
                    sp.wait_ge(max_out, b * GROUPS * DMA + (g + 1) * DMA)
                    sp.dma_start(q_stack[KSPLIT:KSPLIT + 1, r, :, :].rearrange("o j n -> o (j n)"),
                                 max_scr[r].rearrange("(o a) n -> o (a n)", o=1)).then_inc(max_in, DMA)
                sp.wait_ge(h_ready, b + 1)
                sp.dma_start(h_v[b], work[:, :, :]).then_inc(h_out, DMA)
                sp.wait_ge(out_ready, b + 1)
                sp.dma_start(out_v[b], xin[:, :, :]).then_inc(out_written, DMA)
                sp.wait_ge(out_written, b * DMA + DMA)
                sp.wait_ge(h_out, b * DMA + DMA)
                sp.sem_inc(x_free, 1)
            sp.wait_ge(rows_init, 3 * DMA)
            with sp.Fori(0, E // 2) as it:
                for u in range(2):
                    e = it * 2 + u
                    key = ("expert", "ey", u)
                    sp.wait_ge(bank_full[ring.bank(*key)], it * ring.per["expert"] + ring.done(0, *key) - ring.per["expert"])
                    sp.dma_start(e_w1[:, u, :, :], w1_v[e]).then_inc(e_w_in[u], DMA)
                    sp.dma_start(e_w3[:, u, :, :], w3_v[e]).then_inc(e_w_in[u], DMA)
                    sp.dma_start(e_w2[:, u, :, :], w2_v[e]).then_inc(e_w_in[u], DMA)
                    sp.wait_ge(slots_written, B * TT * TOPK * DMA)
                    sp.wait_ge(experts_done, it * 2 + u + 1)
                    sp.dma_start(e_slots[u][:, :], slot_v[e]).then_inc(e_slots_in[u], DMA)

        @block.tensor
        def _(pe):
            def open_tile(it, *key):
                k = ring.bank(*key)
                pe.wait_ge(bank_free[k], ring.done(it, *key))
                return r_ps[k]

            def close(last, *key):
                last.then_inc(bank_full[ring.bank(*key)], 1)

            pe.wait_ge(consts_ready, 1)
            for w, name in enumerate(("wqT", "wpT")):
                pe.wait_ge(w_int_ready, w + 1)
                for c in range(DC):
                    ps = open_tile(0, "setup", name, c)[:, :].bitcast(BF16)
                    for r in range(4):
                        last = nc.tensor.transpose(ps[:, r * P:(r + 1) * P], q_int[:, r, c * P:(c + 1) * P], identb[:, :])
                    close(last, "setup", name, c)
            for w, name in enumerate(("wkT", "wvT")):
                pe.wait_ge(raw_w_in[w], 2 * DMA)
                for c in range(DC):
                    ps = open_tile(0, "setup", name, c)
                    for r in range(4):
                        last = nc.tensor.transpose(ps[:, r * P:(r + 1) * P], probs[:, w, r, c * P:(c + 1) * P], ident[:, :])
                    close(last, "setup", name, c)
            pe.wait_ge(small_in, 8 * DMA)
            ps = open_tile(0, "setup", "gateT")
            for c in range(DC):
                last = nc.tensor.transpose(ps[:, c * E:(c + 1) * E], gate_raw[:, c * P:(c + 1) * P], ident[0:E, 0:E])
            close(last, "setup", "gateT")
            ps = open_tile(0, "setup", "swp")
            for r in range(4):
                last = nc.tensor.matmul(ps[:, r * P:(r + 1) * P], swp[:, r:r + 1].to_broadcast([P, P]), ident[:, :],
                                        start=True, stop=True)
            close(last, "setup", "swp")
            pe.wait_ge(shared_in, 3 * DMA)

            with pe.Fori(0, B) as b:
                def int_transposes(name):
                    for c in range(DC):
                        ps = open_tile(b, "batch", name, c)[:, :].bitcast(BF16)
                        for t in range(TT):
                            last = nc.tensor.transpose(ps[:, t * P:(t + 1) * P], q_int[:, t, c * P:(c + 1) * P], identb[:, :])
                        close(last, "batch", name, c)

                def values(t):
                    pe.wait_ge(ctx_lo_ready, b * KT + t + 1)
                    w = rows(t)
                    ps = open_tile(b, "batch", "v", t)
                    n = 0
                    for a, wt in ((ctx_hi, wkv_hi), (ctx_lo, wkv_hi), (ctx_hi, wkv_lo)):
                        for c in range(DC):
                            last = nc.tensor.matmul(ps[0:w, :], a[:, c, t * P:t * P + w], wt[:, 1, c, :],
                                                    start=(n == 0), stop=(n == 3 * DC - 1))
                            n += 1
                    close(last, "batch", "v", t)

                def prep(key):
                    kind, g = key[0], key[1]
                    r = g % 2
                    ps = open_tile(b, "batch", *key)
                    if kind == "q":
                        for c in range(DC):
                            last = nc.tensor.matmul(ps[:, :], wqT[:, c, g * P:(g + 1) * P], qT_int[:, c, :],
                                                    start=(c == 0), stop=(c == DC - 1))
                    elif kind == "k":
                        at, w = PIECE_AT[key[2]], PIECE[key[2]]
                        n = 0
                        for a, wt in ((ctx_hi, wkv_hi), (ctx_lo, wkv_hi), (ctx_hi, wkv_lo)):
                            for c in range(DC):
                                last = nc.tensor.matmul(ps[:, 0:w], wt[:, 0, c, g * P:(g + 1) * P], a[:, c, at:at + w],
                                                        start=(n == 0), stop=(n == 3 * DC - 1))
                                n += 1
                    elif kind == "max":
                        j, qt, i = key[2:]
                        if (j, qt, i) == (0, 0, 0):
                            pe.wait_ge(stack_in, b * GROUPS * 24 * DMA + (g + 1) * 24 * DMA)
                        at, w = PIECE_AT[i], PIECE[i]
                        last = nc.tensor.matmul(ps[:, 0:w], q_stack[0:KSPLIT, r, j, qt * P:(qt + 1) * P],
                                                k_stack[0:KSPLIT, r, j, at:at + w], start=True, stop=True)
                    else:
                        pe.wait_ge(row_max_ready, b * GROUPS + g + 1)
                        last = nc.tensor.transpose(ps[0:GH * TT, 0:P], row_max[:, :], ident[:, :])
                    close(last, "batch", *key)

                def scores_of(g, kt):
                    w = rows(kt)
                    if kt == 0:
                        pe.wait_ge(max_in, b * GROUPS * DMA + (g + 1) * DMA)
                    for j in range(GH):
                        pe.wait_ge(probs_ready, b * GROUPS * KT * GH + (g * KT + kt) * GH + j + 1)
                        nc.tensor.matmul(s_ps[j][0:w, :], k_stack[:, g % 2, j, kt * P:kt * P + w],
                                         q_stack[:, g % 2, j, :], start=True, stop=True).then_inc(scores_ready, 1)

                def weighted(g, kt):
                    w = rows(kt)
                    if kt == 0:
                        pe.wait_ge(heads_copied, b * GROUPS + g + 1)
                    pe.wait_ge(probs_ready, b * GROUPS * KT * GH + (g * KT + kt + 1) * GH + GH)
                    half = (g * KT + kt) % 2
                    for dst, is_v in ((o_ps, True), (sum_ps, False)):
                        for j in range(GH):
                            h = g * GH + j
                            lhs = v_sb[0:w, kt, h * DH:(h + 1) * DH] if is_v else ones[0:w, :]
                            last = nc.tensor.matmul(dst[j * DH:(j + 1) * DH, :], lhs, probs[0:w, half, j, :],
                                                    start=(kt == 0), stop=(kt == KT - 1))
                    last.then_inc(probs_used, 1)

                def heads_out(g):
                    pe.wait_ge(heads_copied, b * GROUPS + g + 2)
                    ps = open_tile(b, "batch", "oT", g)
                    for t in range(TT):
                        last = nc.tensor.transpose(ps[:, t * P:(t + 1) * P], oT_sb[:, t * P:(t + 1) * P], ident[:, :])
                    close(last, "batch", "oT", g)
                    ps = open_tile(b, "batch", "sumT", g)
                    for t in range(TT):
                        last = nc.tensor.matmul(ps[:, t * GH:(t + 1) * GH], sum_sb[:, t * P:(t + 1) * P],
                                                ident[:, ::DH], start=True, stop=True)
                    close(last, "batch", "sumT", g)

                pe.wait_ge(q_int_ready, b * 2 + 1)
                int_transposes("xT")
                ps = open_tile(b, "batch", "sx")
                for t in range(TT):
                    last = nc.tensor.matmul(ps[:, t * P:(t + 1) * P], sx[:, t:t + 1].to_broadcast([P, P]), ident[:, :],
                                            start=True, stop=True)
                close(last, "batch", "sx")
                for t in range(KT):
                    uses = -(-(KT - t % CT_SLOTS) // CT_SLOTS)
                    pe.wait_ge(ctx_raw_in[t % CT_SLOTS], b * uses * DMA + (t // CT_SLOTS + 1) * DMA)
                    w = rows(t)
                    ps = open_tile(b, "batch", "ctxT", t)
                    for c in range(DC):
                        last = nc.tensor.transpose(ps[:, c * P:c * P + w], ctx_raw[0:w, t % CT_SLOTS, c * P:(c + 1) * P],
                                                   ident[0:w, 0:w])
                    close(last, "batch", "ctxT", t)
                    if t:
                        values(t - 1)
                values(KT - 1)
                pe.wait_ge(evac_act, b * (2 * DC + 1) + DC + 1)
                for key in prep_tiles(0):
                    prep(key)
                for g in range(GROUPS):
                    for kt in range(KT):
                        scores_of(g, kt)
                        if g + 1 < GROUPS:
                            for key in prep_tiles(g + 1, kt):
                                prep(key)
                        if kt == 1 and g:
                            heads_out(g - 1)
                        if kt:
                            weighted(g, kt - 1)
                    weighted(g, KT - 1)
                heads_out(GROUPS - 1)
                pe.wait_ge(q_int_ready, b * 2 + 2)
                int_transposes("oiT")
                pe.wait_ge(evac_act, b * (2 * DC + 1) + 2 * DC + 1)
                for t in range(TT):
                    ps = open_tile(b, "batch", "y", t)
                    for c in range(DC):
                        last = nc.tensor.matmul(ps[:, :], qT_int[:, c, t * P:(t + 1) * P], wpT[:, c, :],
                                                start=(c == 0), stop=(c == DC - 1))
                    close(last, "batch", "y", t)
                pe.wait_ge(h_ready, b + 1)
                for c in range(DC):
                    ps = open_tile(b, "batch", "hT", c)
                    for t in range(TT):
                        last = nc.tensor.transpose(ps[:, t * P:(t + 1) * P], work[:, t, c * P:(c + 1) * P], ident[:, :])
                    close(last, "batch", "hT", c)
                for c in (DC - 2, DC - 1):
                    key = ("batch", "hT", c)
                    pe.wait_ge(free_of(*key), ring.done(b, *key) + 1)
                ps = open_tile(b, "batch", "logits")
                for t in range(TT):
                    for c in range(DC):
                        last = nc.tensor.matmul(ps[:, t * E:(t + 1) * E], hT[:, c, t * P:(t + 1) * P], gateT[:, c, :],
                                                start=(c == 0), stop=(c == DC - 1))
                close(last, "batch", "logits")
                for f in range(FSC):
                    for name, wt in (("gate", sg), ("up", su)):
                        ps = open_tile(b, "batch", name, f)
                        for c in range(DC):
                            last = nc.tensor.matmul(ps[:, :], wt[:, c, f * P:(f + 1) * P], hT[:, c, :],
                                                    start=(c == 0), stop=(c == DC - 1))
                        close(last, "batch", name, f)
                pe.wait_ge(chosen_ready, b + 1)
                ps = open_tile(b, "batch", "cum")
                for t in range(TT):
                    for u in range(t + 1):
                        last = nc.tensor.matmul(ps[:, t * E:(t + 1) * E], tri[:, :] if u == t else onesb[:, :],
                                                chosen[:, u, :], start=(u == 0), stop=(u == t))
                close(last, "batch", "cum")
                ps = open_tile(b, "batch", "total")
                for t in range(TT):
                    last = nc.tensor.matmul(ps[:, 0:E], onesb[:, :], chosen[:, t, :], start=(t == 0), stop=(t == TT - 1))
                close(last, "batch", "total")
                pe.wait_ge(act_ready, b * FSC + FSC)
                for t in range(TT):
                    ps = open_tile(b, "batch", "down", t)
                    for f in range(FSC):
                        last = nc.tensor.matmul(ps[:, :], actT[:, f, t * P:(t + 1) * P], sd[:, f, :],
                                                start=(f == 0), stop=(f == FSC - 1))
                    close(last, "batch", "down", t)
                if ("batch", "even") in ring.n:
                    ps = open_tile(b, "batch", "even")
                    close(nc.tensor.matmul(ps[0:DH, 0:DH], ones[:, :], ones[:, :], start=True, stop=True), "batch", "even")
            with pe.Fori(0, E // 2) as it:
                for u in range(2):
                    pe.wait_ge(e_rows_in[u], it * DMA + DMA)
                    ps = open_tile(it, "expert", "hgT", u)
                    for c in range(DC):
                        last = nc.tensor.transpose(ps[:, c * P:(c + 1) * P], e_rows[u][:, c * P:(c + 1) * P], ident[:, :])
                    close(last, "expert", "hgT", u)
                    pe.wait_ge(e_w_in[u], it * 3 * DMA + 3 * DMA)
                    pe.wait_ge(free_of("expert", "hgT", u), ring.done(it, "expert", "hgT", u) + 1)
                    for name, wt in (("eg", e_w1), ("eu", e_w3)):
                        ps = open_tile(it, "expert", name, u)
                        for f in range(FC):
                            for c in range(DC):
                                last = nc.tensor.matmul(ps[:, f * P:(f + 1) * P], wt[:, u, c, f * P:(f + 1) * P],
                                                        e_rowsT[:, u, c, :], start=(c == 0), stop=(c == DC - 1))
                        close(last, "expert", name, u)
                    pe.wait_ge(e_act_ready, it * 2 + u + 1)
                    ps = open_tile(it, "expert", "ey", u)
                    for f in range(FC):
                        last = nc.tensor.matmul(ps[:, :], e_act[:, u, f, :], e_w2[:, u, f, :],
                                                start=(f == 0), stop=(f == FC - 1))
                    close(last, "expert", "ey", u)

        @block.scalar
        def _(act):
            step = Steps(act, act_step)
            act.wait_ge(small_in, 8 * DMA)
            nc.scalar.activation(tanhs[:, :], tanhs[:, :], ACT.Tanh).then_inc(tanh_ready, 1)
            for w, name in enumerate(("wqT", "wpT")):
                dst = (wqT, wpT)[w]
                for c in range(DC):
                    ps = full(act, 0, "setup", name, c)[:, :].bitcast(BF16)
                    nc.scalar.copy(dst[:, c, :], ps[:, 0:D]).then_inc(free_of("setup", name, c), 1)
            for w, name in enumerate(("wkT", "wvT")):
                for c in range(DC):
                    ps = full(act, 0, "setup", name, c)
                    nc.scalar.copy(wkv_hi[:, w, c, :], ps[:, :]).then_inc(hi_ready, 1)
            ps = full(act, 0, "setup", "gateT")
            nc.scalar.copy(gateT[:, :, :].rearrange("p c e -> p (c e)"), ps[:, 0:DC * E]).then_inc(free_of("setup", "gateT"), 1)
            act.sem_inc(probs_ready, GH)
            act.sem_inc(heads_copied, 1)
            hi_setup = 2 * DC
            hi_per = KT + GROUPS * PIECES

            with act.Fori(0, B) as b:
                step.enter(b, 8)

                def int_copies(name):
                    for c in range(DC):
                        ps = full(act, b, "batch", name, c)[:, :].bitcast(BF16)
                        nc.scalar.copy(qT_int[:, c, :], ps[:, 0:N]).then_inc(evac_act, 1)
                        act.wait_ge(evac_act, b * (2 * DC + 1) + (c + 1 if name == "xT" else DC + 1 + c + 1))
                        act.sem_inc(free_of("batch", name, c), 1)

                def prep(key):
                    kind, g = key[0], key[1]
                    if kind == "k":
                        at, w = PIECE_AT[key[2]], PIECE[key[2]]
                        if key[2] == 0 and (g > 0):
                            act.wait_ge(stack_in, b * GROUPS * 24 * DMA + g * 24 * DMA)
                        ps = full(act, b, "batch", *key)
                        nc.scalar.activation(k_hi[:, at:at + w], ps[:, 0:w], ACT.Identity,
                                             bias=bk_col[:, g:g + 1]).then_inc(hi_ready, 1)
                    elif kind == "maxT":
                        ps = full(act, b, "batch", *key)
                        nc.scalar.mul(max_row[:, :], ps[0:GH * TT, 0:P], -1.0).then_inc(max_row_ready, 1)
                        act.wait_ge(max_row_ready, b * GROUPS + g + 1)
                        act.sem_inc(free_of("batch", *key), 1)

                def exps(g, kt):
                    w = rows(kt)
                    half = (g * KT + kt) % 2
                    act.wait_ge(probs_used, b * GROUPS * KT + g * KT + kt + 1)
                    for j in range(GH):
                        act.wait_ge(scores_ready, b * GROUPS * KT * GH + (g * KT + kt) * GH + j + 1)
                        nc.scalar.activation(probs[0:w, half, j, :], s_ps[j][0:w, :], ACT.Exp).then_inc(probs_ready, 1)

                def copy_heads(g):
                    act.wait_ge(probs_used, b * GROUPS * KT + (g + 1) * KT + 2)
                    step.mark(nc.scalar.copy(oT_sb[:, :], o_ps[:, :]))
                    nc.scalar.copy(sum_sb[:, :], sum_ps[:, :]).then_inc(heads_copied, 1)

                act.wait_ge(var_ready, b * 2 + 1)
                nc.scalar.activation(std[:, :], mv[:, :, 1], ACT.Sqrt, bias=eps[:, :]).then_inc(std_ready, 1)
                int_copies("xT")
                ps = full(act, b, "batch", "sx")
                nc.scalar.copy(sx_row[:, :], ps[:, :]).then_inc(evac_act, 1)
                act.wait_ge(evac_act, b * (2 * DC + 1) + DC + 1)
                act.sem_inc(free_of("batch", "sx"), 1)
                for t in range(KT):
                    w = rows(t)
                    ps = full(act, b, "batch", "ctxT", t)
                    nc.scalar.copy(ctx_hi[:, :, t * P:t * P + w],
                                   ps[:, :].rearrange("p (c m) -> p c m", c=DC)[:, :, 0:w]).then_inc(hi_ready, 1)
                for key in prep_tiles(0):
                    prep(key)
                for g in range(GROUPS):
                    for kt in range(KT):
                        exps(g, kt)
                        if g + 1 < GROUPS:
                            for key in prep_tiles(g + 1, kt):
                                prep(key)
                    copy_heads(g)
                int_copies("oiT")
                act.wait_ge(var_ready, b * 2 + 2)
                nc.scalar.activation(std[:, :], mv[:, :, 1], ACT.Sqrt, bias=eps[:, :]).then_inc(std_ready, 1)
                for c in range(DC):
                    ps = full(act, b, "batch", "hT", c)
                    nc.scalar.copy(hT[:, c, :], ps[:, :]).then_inc(free_of("batch", "hT", c), 1)
                ps = full(act, b, "batch", "logits")
                nc.scalar.activation(scores[:, :, :].rearrange("p t e -> p (t e)"), ps[:, 0:TT * E],
                                     ACT.Sigmoid).then_inc(scores_sig, 1)
                act.wait_ge(scores_sig, b + 1)
                act.sem_inc(free_of("batch", "logits"), 1)
                for f in range(FSC):
                    ps = full(act, b, "batch", "gate", f)
                    if f:
                        act.wait_ge(act_ready, b * FSC + f)
                    nc.scalar.activation(sig[:, :], ps[:, :], ACT.Sigmoid).then_inc(sig_ready, 1)
                step.leave(B)
            with act.Fori(0, E // 2) as it:
                for u in range(2):
                    ps = full(act, it, "expert", "hgT", u)
                    nc.scalar.copy(e_rowsT[:, u, :, :].rearrange("p c n -> p (c n)"), ps[:, :]
                                   ).then_inc(free_of("expert", "hgT", u), 1)
                    ps = full(act, it, "expert", "eg", u)
                    nc.scalar.activation(e_sig[:, :], ps[:, 0:FC * P], ACT.Sigmoid).then_inc(e_sig_ready, 1)

        @block.vector
        def _(dve):
            step = Steps(dve, dve_step, dve_wait_carrier)
            V = nc.vector

            def quantise(src, scale_out):
                step.mark(V.tensor_reduce(out=amax[:, :], in_=src[:, :, :], op=ALU.max, axis=X_AXIS, apply_absolute_value=True))
                step.settle()
                step.mark(V.tensor_scalar(scale_out[:, :], amax[:, :], 1.0 / 127.0, 1e-8, ALU.mult, ALU.max))
                step.settle()
                step.mark(V.reciprocal(inv[:, :], scale_out[:, :]))
                step.settle()
                for t in range(TT):
                    step.mark(V.tensor_scalar(src[:, t, :], src[:, t, :], inv[:, t:t + 1], 127.0, ALU.mult, ALU.min))
                step.settle()
                for t in range(TT):
                    step.mark(V.tensor_scalar(src[:, t, :], src[:, t, :], -127.0, ROUND, ALU.max, ALU.add))
                step.settle()
                for t in range(TT):
                    last = V.tensor_scalar(q_int[:, t, :], src[:, t, :], ROUND, None, ALU.subtract)
                    if t < TT - 1:
                        step.mark(last)
                return last

            dve.sem_inc(bank_free[0], 1)
            dve.sem_inc(bank_free[1], 1)
            dve.sem_inc(probs_used, 2)
            dve.sem_inc(x_free, 1)
            step.mark(V.memset(carry[:, :], 0.0))
            step.mark(V.memset(gsum[:, :, :], -3.0e38))
            step.mark(V.memset(k_stack[KSPLIT:KSPLIT + 1, :, :, :], 1.0))
            for w, scale in enumerate((swq, swp)):
                dve.wait_ge(raw_w_in[w], DMA)
                if w:
                    full(dve, 0, "setup", "wqT", DC - 1)
                    full(dve, 0, "setup", "wqT", DC - 2)
                quantise(probs[:, w], scale).then_inc(w_int_ready, 1)
            for w, name in enumerate(("wkT", "wvT")):
                for c in range(DC):
                    ps = full(dve, 0, "setup", name, c)
                    dve.wait_ge(hi_ready, w * DC + c + 1)
                    V.tensor_tensor(wkv_lo[:, w, c, :], ps[:, :], wkv_hi[:, w, c, :], ALU.subtract
                                    ).then_inc(free_of("setup", name, c), 1)
            dve.wait_ge(tanh_ready, 1)
            dve.wait_ge(rows_init, 3 * DMA)
            ps = full(dve, 0, "setup", "swp")
            V.tensor_scalar(swp_row[:, :], ps[:, :], tanhs[:, 0:1], None, ALU.mult).then_inc(free_of("setup", "swp"), 1)
            step.mark(V.tensor_scalar(bq_col[:, :], bq_col[:, :], SCALE, None, ALU.mult))
            V.tensor_scalar(bp_row[:, :], bp_row[:, :], tanhs[:, 0:1], None, ALU.mult).then_inc(row_consts_ready, 1)
            hi_setup, hi_per = 2 * DC, KT + GROUPS * PIECES

            with dve.Fori(0, B) as b:
                step.enter(b, 400)

                def layernorm(n):
                    for t in range(TT):
                        step.mark(V.bn_stats(stats[:, t, :], xin[:, t, :]))
                    step.settle()
                    step.carry_wait()
                    for t in range(TT):
                        last = V.bn_aggr(mv[:, t, :], stats[:, t, :])
                        if t < TT - 1:
                            step.mark(last)
                    last.then_inc(var_ready, 1)
                    dve.wait_ge(std_ready, b * 2 + n)
                    step.mark(V.reciprocal(rstd[:, :], std[:, :]))
                    step.settle()
                    for t in range(TT):
                        last = V.tensor_scalar(work[:, t, :], xin[:, t, :], mv[:, t, 0:1], rstd[:, t:t + 1],
                                               ALU.subtract, ALU.mult)
                        if t < TT - 1 or n == 1:
                            step.mark(last)
                    return last

                def prep(key):
                    kind, g = key[0], key[1]
                    if kind == "q":
                        if g:
                            dve.wait_ge(stack_in, b * GROUPS * 24 * DMA + g * 24 * DMA)
                        ps = full(dve, b, "batch", *key)
                        V.scalar_tensor_tensor(out=qf[:, :], in0=ps[:, :], scalar=swq[:, g:g + 1], in1=sx_row[:, :],
                                               op0=ALU.mult, op1=ALU.mult).then_inc(free_of("batch", *key), 1)
                        dve.wait_ge(free_of("batch", *key), ring.done(b, "batch", *key) + 1)
                        step.mark(V.tensor_scalar(qf[:, :], qf[:, :], SCALE, bq_col[:, g:g + 1], ALU.mult, ALU.add))
                        step.settle()
                        step.mark(V.tensor_copy(q_hi[:, :], qf[:, :]))
                        step.settle()
                        V.tensor_tensor(q_lo[:, :], qf[:, :], q_hi[:, :], ALU.subtract).then_inc(q_split, 1)
                    elif kind == "k":
                        i = key[2]
                        at, w = PIECE_AT[i], PIECE[i]
                        dve.wait_ge(hi_ready, b * hi_per + hi_setup + KT + g * PIECES + i + 1)
                        k = ring.bank("batch", *key)
                        V.scalar_tensor_tensor(out=k_lo[:, at:at + w], in0=r_ps[k][:, 0:w], scalar=bk_col[:, g:g + 1],
                                               in1=k_hi[:, at:at + w], op0=ALU.add, op1=ALU.subtract
                                               ).then_inc(free_of("batch", *key), 1)
                        if i == PIECES - 1:
                            dve.wait_ge(free_of("batch", *key), ring.done(b, "batch", *key) + 1)
                            dve.sem_inc(k_split, 1)
                    elif kind == "max":
                        j, qt, i = key[2:]
                        ps = full(dve, b, "batch", *key)
                        V.reduce_max(piece_max[:, j * TT + qt, i:i + 1], ps[:, 0:PIECE[i]], X_AXIS
                                     ).then_inc(free_of("batch", *key), 1)
                        if (j, qt, i) == (GH - 1, TT - 1, PIECES - 1):
                            dve.wait_ge(free_of("batch", *key), ring.done(b, "batch", *key) + 1)
                            V.reduce_max(row_max[:, :], piece_max[:, :, :], X_AXIS).then_inc(row_max_ready, 1)

                def heads_out(g):
                    po = full(dve, b, "batch", "oT", g)
                    pss = full(dve, b, "batch", "sumT", g)
                    V.reciprocal(rsum[:, :, :].rearrange("p t j -> p (t j)"), pss[:, 0:TT * GH]
                                 ).then_inc(free_of("batch", "sumT", g), 1)
                    dve.wait_ge(free_of("batch", "sumT", g), ring.done(b, "batch", "sumT", g) + 1)
                    for t in range(TT):
                        last = V.tensor_tensor(
                            work[:, t, g * P:(g + 1) * P].rearrange("p (j d) -> p j d", j=GH),
                            po[:, t * P:(t + 1) * P].rearrange("p (j d) -> p j d", j=GH),
                            rsum[:, t, :].unsqueeze(2).to_broadcast([P, GH, DH]), ALU.mult)
                        if t < TT - 1:
                            step.mark(last)
                    last.then_inc(free_of("batch", "oT", g), 1)
                    dve.wait_ge(free_of("batch", "oT", g), ring.done(b, "batch", "oT", g) + 1)

                dve.wait_ge(x_in, b * DMA + DMA)
                layernorm(1)
                step.settle()
                quantise(work, sx).then_inc(q_int_ready, 1)
                def value_tile(t):
                    w = rows(t)
                    ps = full(dve, b, "batch", "v", t)
                    V.tensor_tensor(v_sb[0:w, t, :], ps[0:w, :], bv_row[0:w, :], ALU.add).then_inc(free_of("batch", "v", t), 1)

                for t in range(KT):
                    w = rows(t)
                    dve.wait_ge(hi_ready, b * hi_per + hi_setup + t + 1)
                    ps = r_ps[ring.bank("batch", "ctxT", t)]
                    V.tensor_tensor(ctx_lo[:, :, t * P:t * P + w],
                                    ps[:, :].rearrange("p (c m) -> p c m", c=DC)[:, :, 0:w],
                                    ctx_hi[:, :, t * P:t * P + w], ALU.subtract).then_inc(ctx_lo_ready, 1)
                    dve.wait_ge(ctx_lo_ready, b * KT + t + 1)
                    dve.sem_inc(free_of("batch", "ctxT", t), 1)
                    if t:
                        value_tile(t - 1)
                value_tile(KT - 1)
                for key in prep_tiles(0):
                    prep(key)
                for g in range(GROUPS):
                    for kt in range(KT):
                        if g + 1 < GROUPS:
                            for key in prep_tiles(g + 1, kt):
                                prep(key)
                        if kt == 1 and g:
                            heads_out(g - 1)
                heads_out(GROUPS - 1)
                quantise(work, so).then_inc(q_int_ready, 1)
                dve.wait_ge(x_biased, b + 1)
                for t in range(TT):
                    ps = full(dve, b, "batch", "y", t)
                    V.scalar_tensor_tensor(out=work[:, t, :], in0=ps[:, :], scalar=so[:, t:t + 1], in1=swp_row[:, :],
                                           op0=ALU.mult, op1=ALU.mult).then_inc(free_of("batch", "y", t), 1)
                    dve.wait_ge(free_of("batch", "y", t), ring.done(b, "batch", "y", t) + 1)
                    step.mark(V.tensor_tensor(xin[:, t, :], xin[:, t, :], work[:, t, :], ALU.add))
                step.settle()
                layernorm(2).then_inc(h_ready, 1)

                dve.wait_ge(scores_sig, b + 1)
                step.mark(V.tensor_tensor(biased[:, :, :], scores[:, :, :],
                                          gbias[:, :].unsqueeze(1).to_broadcast([P, TT, E]), ALU.add))
                step.settle()
                step.carry_wait()
                for t in range(TT):
                    for q in range(EGROUPS):
                        step.mark(V.max(top8[:, t, q, :], biased[:, t, q * EPG:(q + 1) * EPG]))
                step.settle()
                step.mark(V.tensor_tensor(gsum[:, :, 0:EGROUPS], top8[:, :, :, 0], top8[:, :, :, 1], ALU.add))
                step.settle()
                step.carry_wait()
                for t in range(TT):
                    step.mark(V.max(gtop[:, t, :], gsum[:, t, :]))
                step.settle()
                step.carry_wait()
                for t in range(TT):
                    step.mark(V.max_index(gidx[:, t, :], gtop[:, t, :], gsum[:, t, :]))
                step.settle()
                step.mark(V.tensor_copy(gidxf[:, :, :], gidx[:, :, 0:2]))
                step.settle()
                for k in range(2):
                    step.mark(V.tensor_tensor(geq[:, :, k, :], lane[:, 0:EGROUPS].unsqueeze(1).to_broadcast([P, TT, EGROUPS]),
                                              gidxf[:, :, k:k + 1].to_broadcast([P, TT, EGROUPS]), ALU.is_equal))
                step.settle()
                step.mark(V.tensor_tensor(gmask[:, :, :], geq[:, :, 0, :], geq[:, :, 1, :], ALU.add))
                step.settle()
                step.mark(V.tensor_tensor(masked[:, :, :].rearrange("p t (q e) -> p (t q) e", q=EGROUPS),
                                          biased[:, :, :].rearrange("p t (q e) -> p (t q) e", q=EGROUPS),
                                          gmask[:, :, :].rearrange("p t q -> p (t q)").unsqueeze(2).to_broadcast([P, TT * EGROUPS, EPG]),
                                          ALU.mult))
                step.settle()
                step.carry_wait()
                for t in range(TT):
                    step.mark(V.max(etop[:, t, :], masked[:, t, :]))
                step.settle()
                step.carry_wait()
                for t in range(TT):
                    step.mark(V.max_index(eidx[:, t, :], etop[:, t, :], masked[:, t, :]))
                step.settle()
                step.mark(V.tensor_copy(eidxf[:, :, :], eidx[:, :, 0:TOPK]))
                step.settle()
                for t in range(TT):
                    step.mark(V.tensor_tensor(onehot[:, t, :, :], lane[:, :].unsqueeze(1).to_broadcast([P, TOPK, E]),
                                              eidxf[:, t, :].unsqueeze(2).to_broadcast([P, TOPK, E]), ALU.is_equal))
                step.settle()
                with nc.allow_low_precision("counts of 0 and 1") if hasattr(nc, "allow_low_precision") else ExitStack():
                    V.tensor_reduce(out=chosen[:, :, :], in_=onehot[:, :, :, :].rearrange("p t k e -> p t e k"),
                                    op=ALU.add, axis=X_AXIS).then_inc(chosen_ready, 1)
                for t in range(TT):
                    step.mark(V.tensor_tensor(picked[:, t, :, :], onehot[:, t, :, :],
                                              scores[:, t, :].unsqueeze(1).to_broadcast([P, TOPK, E]), ALU.mult))
                step.settle()
                step.mark(V.tensor_reduce(out=wk[:, :, :], in_=picked[:, :, :, :], op=ALU.add, axis=X_AXIS))
                step.settle()
                step.mark(V.tensor_reduce(out=wsum[:, :], in_=wk[:, :, :], op=ALU.add, axis=X_AXIS))
                step.settle()
                step.mark(V.tensor_scalar(wsum[:, :], wsum[:, :], 1e-20, None, ALU.add))
                step.settle()
                step.mark(V.reciprocal(wrec[:, :], wsum[:, :]))
                step.settle()
                dve.wait_ge(payload_free, b + 1)
                for t in range(TT):
                    step.mark(V.tensor_scalar(payload[:, t, :, 1], wk[:, t, :], wrec[:, t:t + 1], 2.0, ALU.mult, ALU.mult))
                step.settle()

                def swiglu(f):
                    dve.wait_ge(sig_ready, b * FSC + f + 1)
                    pg = r_ps[ring.bank("batch", "gate", f)]
                    V.tensor_tensor(gsil[:, :], pg[:, :], sig[:, :], ALU.mult).then_inc(free_of("batch", "gate", f), 1)
                    dve.wait_ge(free_of("batch", "gate", f), ring.done(b, "batch", "gate", f) + 1)
                    pu = full(dve, b, "batch", "up", f)
                    V.tensor_tensor(actT[:, f, :], pu[:, :], gsil[:, :], ALU.mult).then_inc(act_ready, 1)
                    dve.wait_ge(act_ready, b * FSC + f + 1)
                    dve.sem_inc(free_of("batch", "up", f), 1)

                for f in range(FSC):
                    swiglu(f)
                ps = full(dve, b, "batch", "cum")
                V.tensor_tensor(cum[:, :, :], ps[:, 0:TT * E].rearrange("p (t e) -> p t e", t=TT),
                                carry[:, :].unsqueeze(1).to_broadcast([P, TT, E]), ALU.add).then_inc(free_of("batch", "cum"), 1)
                dve.wait_ge(free_of("batch", "cum"), ring.done(b, "batch", "cum") + 1)
                ps = full(dve, b, "batch", "total")
                V.tensor_tensor(carry[:, :], ps[:, 0:E], carry[:, :], ALU.add).then_inc(free_of("batch", "total"), 1)
                for t in range(TT):
                    step.mark(V.tensor_tensor(picked[:, t, :, :], onehot[:, t, :, :],
                                              cum[:, t, :].unsqueeze(1).to_broadcast([P, TOPK, E]), ALU.mult))
                step.settle()
                step.mark(V.tensor_reduce(out=pos[:, :, :], in_=picked[:, :, :, :], op=ALU.add, axis=X_AXIS))
                step.settle()
                step.mark(V.tensor_scalar(over[:, :, :], pos[:, :, :], float(CAP), float(2 * E * CAP), ALU.is_ge, ALU.mult))
                step.mark(V.scalar_tensor_tensor(out=slotf[:, :, :], in0=eidxf[:, :, :], scalar=float(CAP), in1=pos[:, :, :],
                                                 op0=ALU.mult, op1=ALU.add))
                step.settle()
                V.tensor_tensor(slot[:, :, :], slotf[:, :, :], over[:, :, :], ALU.add).then_inc(route_ready, 1)
                for t in range(TT):
                    ps = full(dve, b, "batch", "down", t)
                    V.scalar_tensor_tensor(out=xin[:, t, :], in0=ps[:, :], scalar=tanhs[:, 1:2], in1=xin[:, t, :],
                                           op0=ALU.mult, op1=ALU.add).then_inc(free_of("batch", "down", t), 1)
                dve.wait_ge(free_of("batch", "down", TT - 1), ring.done(b, "batch", "down", TT - 1) + 1)
                dve.sem_inc(out_ready, 1)
                if ("batch", "even") in ring.n:
                    full(dve, b, "batch", "even")
                    dve.sem_inc(free_of("batch", "even"), 1)
                step.leave(B)
            with dve.Fori(0, E // 2) as it:
                for u in range(2):
                    dve.wait_ge(e_sig_ready, it * 2 + u + 1)
                    pg = r_ps[ring.bank("expert", "eg", u)]
                    key = ("expert", "eg", u)
                    V.tensor_tensor(e_gsil[:, :], pg[:, 0:FC * P], e_sig[:, :], ALU.mult).then_inc(free_of(*key), 1)
                    dve.wait_ge(free_of(*key), ring.done(it, *key) + 1)
                    pu = full(dve, it, "expert", "eu", u)
                    V.tensor_tensor(e_act[:, u, :, :].rearrange("p f n -> p (f n)"), pu[:, 0:FC * P], e_gsil[:, :], ALU.mult
                                    ).then_inc(e_act_ready, 1)
                    dve.wait_ge(e_act_ready, it * 2 + u + 1)
                    dve.sem_inc(free_of("expert", "eu", u), 1)
                    dve.wait_ge(e_slots_in[u], it * DMA + DMA)
                    dve.wait_ge(experts_done, it * 2 + u + 1)
                    ps = full(dve, it, "expert", "ey", u)
                    V.tensor_scalar(e_y[u][:, :], ps[:, :], e_slots[u][:, 1:2], tanhs[:, 1:2], ALU.mult, ALU.mult
                                    ).then_inc(e_y_ready, 1)
                    dve.wait_ge(e_y_ready, it * 2 + u + 1)
                    dve.sem_inc(free_of("expert", "ey", u), 1)

        @block.gpsimd
        def _(pool):
            step = Steps(pool, pool_step, pool_wait_carrier)
            G = nc.gpsimd
            for m in (ident, identb):
                step.mark(G.memset(m[:, :], 0.0))
            for m, v in ((onesb, 1.0), (ones, 1.0), (tri, 1.0), (eps, EPS), (zero_rows, 0.0), (slot_init, 0.0)):
                ap = m[:, :, :] if m is slot_init else m[:, :]
                step.mark(G.memset(ap, v))
            step.mark(G.iota(lane[:, :], [[1, E]], base=0, channel_multiplier=0, allow_small_or_imprecise_dtypes=True))
            step.settle()
            for m in (ident, identb):
                step.mark(G.affine_select(out=m[:, :], in_=m[:, :], compare_op=ALU.not_equal, fill=1.0, base=0,
                                          pattern=[[-1, P]], channel_multiplier=1))
            step.mark(G.affine_select(out=tri[:, :], in_=tri[:, :], compare_op=ALU.is_gt, fill=0.0, base=0,
                                      pattern=[[1, P]], channel_multiplier=-1))
            step.mark(G.iota(slot_init[:, :, 0].bitcast(I32), [[0, E]], base=TOK, channel_multiplier=1))
            step.settle()
            pool.sem_inc(consts_ready, 1)
            pool.sem_inc(payload_free, 1)
            pool.sem_inc(experts_done, 2)
            step.mark(G.iota(token[:, :, :], [[P, TT], [0, TOPK]], base=0, channel_multiplier=1,
                             allow_small_or_imprecise_dtypes=True))
            pool.wait_ge(row_consts_ready, 1)
            pool.wait_ge(rows_init, 3 * DMA)
            with pool.Fori(0, B) as b:
                step.enter(b, 8)
                pool.wait_ge(q_int_ready, b * 2 + 1)
                for t in range(TT):
                    last = G.tensor_tensor(xin[:, t, :], xin[:, t, :], bp_row[:, :], ALU.add)
                    if t < TT - 1:
                        step.mark(last)
                last.then_inc(x_biased, 1)
                pool.wait_ge(payload_free, b + 1)
                step.settle()
                step.carry_wait()
                step.mark(G.tensor_copy(payload_i[:, :, :, 0], token[:, :, :]))
                step.settle()
                step.carry_wait()
                step.mark(G.tensor_scalar(token[:, :, :], token[:, :, :], float(N), None, ALU.add))
                pool.wait_ge(route_ready, b + 1)
                step.carry_wait()
                for t in range(TT):
                    for k in range(TOPK):
                        G.indirect_dma_start(out=slot_scr, out_offset=bass.IndirectOffsetOnAxis(ap=slot[:, t, k:k + 1], axis=0),
                                             in_=payload[:, t, k, :], in_offset=None, bounds_check=E * CAP - 1,
                                             oob_is_err=False).then_inc(slots_written, DMA)
                        pool.wait_ge(slots_written, b * TT * TOPK * DMA + (t * TOPK + k + 1) * DMA)
                        step.carry_wait()
                pool.sem_inc(payload_free, 1)
                step.leave(B)
            pool.wait_ge(h_out, B * DMA)
            pool.wait_ge(out_written, B * DMA)

            def gather(it, u):
                pool.wait_ge(e_slots_in[u], it * DMA + DMA)
                key = ("expert", "hgT", u)
                pool.wait_ge(bank_full[ring.bank(*key)], it * ring.per["expert"] + ring.done(0, *key) - ring.per["expert"])
                step.carry_wait()
                G.indirect_dma_start(out=e_rows[u][:, :], out_offset=None, in_=h_scr,
                                     in_offset=bass.IndirectOffsetOnAxis(ap=e_slots[u][:, 0:1].bitcast(I32), axis=0),
                                     bounds_check=TOK + CAP - 1, oob_is_err=True).then_inc(e_rows_in[u], DMA)

            def add_rows(it, u):
                pool.wait_ge(e_y_ready, it * 2 + u + 1)
                step.carry_wait()
                G.indirect_dma_start(out=out, out_offset=bass.IndirectOffsetOnAxis(ap=e_slots[u][:, 0:1].bitcast(I32), axis=0),
                                     in_=e_y[u][:, :], in_offset=None, bounds_check=TOK + CAP - 1, oob_is_err=True,
                                     compute_op=ALU.add).then_inc(rows_added, DMA)

            def finish(it, u):
                pool.wait_ge(rows_added, it * 2 * DMA + (u + 1) * DMA)
                pool.sem_inc(experts_done, 1)

            gather(0, 0)
            gather(0, 1)
            add_rows(0, 0)
            with pool.Fori(0, E // 2 - 1) as it:
                finish(it, 0)
                gather(it + 1, 0)
                add_rows(it, 1)
                finish(it, 1)
                gather(it + 1, 1)
                add_rows(it + 1, 0)
            finish(E // 2 - 1, 0)
            add_rows(E // 2 - 1, 1)
            finish(E // 2 - 1, 1)


_INS = ["x", "ctx_2048", "g_xattn", "g_ffn", "L0_xattn_wq", "L0_xattn_bq", "L0_xattn_wkv", "L0_xattn_bkv",
        "L0_xattn_wp", "L0_xattn_bp", "L0_ffn_gate_w", "L0_ffn_gate_bias", "L0_ffn_w1", "L0_ffn_w2", "L0_ffn_w3",
        "L0_ffn_shared_gate", "L0_ffn_shared_up", "L0_ffn_shared_down"]


def kernel(**inputs):
    import numpy as np
    import concourse.bacc as bacc
    from concourse.bass_utils import run_bass_kernel_spmd

    nc = bacc.Bacc("TRN2", target_bir_lowering=False, num_devices=1)
    arrays, args = {}, []
    for name in _INS:
        a = np.ascontiguousarray(inputs[name])
        arrays[f"in_{name}"] = a
        args.append(nc.dram_tensor(f"in_{name}", a.shape, mybir.dt.from_np(a.dtype), kind="ExternalInput").ap())
    out = nc.dram_tensor("out_rows", (TOK + CAP, D), FP32, kind="ExternalOutput").ap()
    by = dict(zip(_INS, args))
    build(nc, by["x"], by["ctx_2048"], by["g_xattn"], by["g_ffn"], by["L0_xattn_wq"], by["L0_xattn_bq"],
          by["L0_xattn_wkv"], by["L0_xattn_bkv"], by["L0_xattn_wp"], by["L0_xattn_bp"], by["L0_ffn_gate_w"],
          by["L0_ffn_gate_bias"], by["L0_ffn_w1"], by["L0_ffn_w2"], by["L0_ffn_w3"], by["L0_ffn_shared_gate"],
          by["L0_ffn_shared_up"], by["L0_ffn_shared_down"], out)
    r = run_bass_kernel_spmd(nc, [arrays], core_ids=[0])
    return r.results[0]["out_rows"][0:TOK].reshape(B, N, D)
```

```python
from contextlib import ExitStack

import concourse.bass as bass
from concourse import mybir

FP32, FP16, BF16, I32, U32 = (mybir.dt.float32, mybir.dt.float16, mybir.dt.bfloat16,
                              mybir.dt.int32, mybir.dt.uint32)
ALU = mybir.AluOpType
ACT = mybir.ActivationFunctionType
X_AXIS = mybir.AxisListType.X

B, N, D = 8, 512, 512
M = 1601
HEADS, DH = 16, 32
P = 128
TT = N // P
DC = D // P
KT = (M + P - 1) // P
GROUPS, GH = 4, 4
PIECES = 4
PIECE = [M // PIECES + (1 if i < M % PIECES else 0) for i in range(PIECES)]
PIECE_AT = [sum(PIECE[:i]) for i in range(PIECES)]
E, TOPK, EGROUPS, EPG, CAP, F, FS = 32, 4, 4, 8, 128, 256, 512
TOK = B * N
FSC, FC = FS // P, F // P
KSPLIT = 3 * DH
SCALE = 1.0 / float(DH) ** 0.5
EPS = 1e-5
ROUND = 12582912.0
CT_SLOTS = 3
V_EARLY = min(6, (KT - 1) // 2)
V_LATE = 4
VAR_AT = 5
UN = 4
DMA = 16


def rows(t):
    return min(P, M - t * P)


def prep_tiles(g, step=None):
    score_max = [("max", g, j, qt, i) for j in range(GH) for qt in range(TT) for i in range(PIECES)]
    at = [[] for _ in range(KT)]
    at[0] = [("q", g)] + [("k", g, i) for i in range(PIECES // 2)]
    at[1] = [("k", g, i) for i in range(PIECES // 2, PIECES)]
    first, last = 3, KT - 2
    per = -(-len(score_max) // (last - first))
    for s in range(first, last):
        at[s] = score_max[(s - first) * per:(s - first + 1) * per]
    at[last] = [("maxT", g)]
    return at[step] if step is not None else [t for s in at for t in s]


def first_keys():
    return [key for key in prep_tiles(0) if key[0] == "k"]


def first_queries():
    left = [("v", t) for t in range(V_EARLY, KT - V_LATE)]
    return prep_tiles(0)[0:1] + left + [key for key in prep_tiles(0)[1:] if key[0] != "k"]


def values_after(t):
    return t // 2 - 1 if t % 2 == 0 and 0 <= t // 2 - 1 < V_EARLY else None


def setup_order():
    return ([("wqT", c) for c in range(DC)] + [("wpT", c) for c in range(DC)]
            + [("wkT", c) for c in range(DC)] + [("wvT", c) for c in range(DC)]
            + [("gateT",), ("swp",)])


def batch_order():
    order = []
    for t in range(KT):
        order.append(("ctxT", t))
        if values_after(t) is not None:
            order.append(("v", values_after(t)))
    order += first_keys()
    order += [("xT", c) for c in range(DC)] + [("sx",)]
    order += first_queries()
    for g in range(GROUPS):
        for kt in range(KT):
            if g + 1 < GROUPS:
                order += prep_tiles(g + 1, kt)
            if kt == 1 and g:
                order += [("oT", g - 1), ("sumT", g - 1)]
    order += [("oT", GROUPS - 1), ("sumT", GROUPS - 1)]
    order += [("oiT", c) for c in range(DC)] + [("y", t) for t in range(TT)]
    order += [("hT", c) for c in range(DC)] + [("logits",)]
    for f in range(FSC):
        order += [("gate", f), ("up", f)]
    order += [("cum",), ("total",)]
    order += [("down", t) for t in range(TT)]
    if len(order) % 2:
        order.append(("even",))
    return order


def expert_order():
    order = [("hgT", 0)]
    for u in range(UN):
        order += [("eg", u), ("eu", u)] + ([("hgT", u + 1)] if u + 1 < UN else []) + [("ey", u)]
    return order


class Ring:

    def __init__(self):
        self.n, self.base, self.per, at = {}, {}, {}, 0
        for stage, order, times in (("setup", setup_order(), 1), ("batch", batch_order(), B),
                                    ("expert", expert_order(), E // UN)):
            assert len(order) % 2 == 0 and len(set(order)) == len(order)
            for i, key in enumerate(order):
                self.n[(stage,) + key] = i
            self.base[stage], self.per[stage] = at // 2, len(order) // 2
            at += len(order) * times

    def bank(self, *key):
        return self.n[key] % 2

    def done(self, it, *key):
        stage = key[0]
        k = self.base[stage] + self.n[key] // 2 + 1
        return k if stage == "setup" else it * self.per[stage] + k


class Steps:

    def __init__(self, engine, sem, wait_carrier=None):
        self.engine, self.sem, self.wait_carrier = engine, sem, wait_carrier
        self.base, self.k, self.it, self.per = 0, 0, None, 0

    def mark(self, instruction):
        self.k += 1
        instruction.then_inc(self.sem, 1)

    def value(self):
        return self.base + self.k if self.it is None else self.it * self.per + (self.base + self.k)

    def settle(self):
        self.engine.wait_ge(self.sem, self.value())

    def carry_wait(self):
        self.engine.sem_inc(self.wait_carrier, 1)

    def enter(self, it, per):
        self.base, self.k, self.it, self.per = self.base + self.k, 0, it, per

    def leave(self, times):
        assert self.k <= self.per, (self.k, self.per)
        self.settle()
        if self.k < self.per:
            self.engine.sem_inc(self.sem, self.per - self.k)
        self.base, self.k, self.it = self.base + self.per * times, 0, None


def build(nc, x, ctx_in, g_xattn, g_ffn, wq, bq, wkv, bkv, wp, bp, gate_w, gate_bias, w1, w2, w3,
          shared_gate, shared_up, shared_down, out):
    x_v = x.rearrange("b (t p) d -> b p t d", p=P)
    out_v = out[0:TOK, :].rearrange("(b t p) d -> b p t d", p=P, t=TT)
    h_scr = nc.dram_tensor("h_rows", [TOK + CAP, D], FP32).ap()
    h_v = h_scr[0:TOK, :].rearrange("(b t p) d -> b p t d", p=P, t=TT)
    slot_scr = nc.dram_tensor("slot_rows", [E * CAP, 2], FP32).ap()
    slot_v = slot_scr.rearrange("(e c) w -> e c w", c=CAP)
    w1_v = w1.rearrange("e (c p) f -> e p c f", p=P)
    w3_v = w3.rearrange("e (c p) f -> e p c f", p=P)
    w2_v = w2.rearrange("e (c p) d -> e p c d", p=P)
    max_scr = nc.dram_tensor("max_rows", [2, GH * TT, P], FP16).ap()
    ring = Ring()

    ctx = ExitStack()
    with ctx:
        def sb(name, shape, dt):
            return ctx.enter_context(nc.sbuf_tensor(name, shape, dt))

        def sem(name):
            return ctx.enter_context(nc.semaphore(name))

        ident = sb("ident", [P, P], FP32)
        identb = sb("identb", [P, P], BF16)
        tri = sb("tri", [P, P], BF16)
        onesb = sb("onesb", [P, P], BF16)
        ones = sb("ones", [P, DH], FP32)
        lane = sb("lane", [P, E], FP32)
        eps = sb("eps", [P, 1], FP32)
        wqT = sb("wqT", [P, DC, D], BF16)
        wpT = sb("wpT", [P, DC, D], BF16)
        wkv_hi = sb("wkv_hi", [P, 2, DC, D], FP16)
        wkv_lo = sb("wkv_lo", [P, 2, DC, D], FP16)
        sg = sb("sg", [P, DC, FS], FP32)
        su = sb("su", [P, DC, FS], FP32)
        sd = sb("sd", [P, FSC, D], FP32)
        gateT = sb("gateT", [P, DC, E], FP32)
        gbias = sb("gbias", [P, E], FP32)
        swq = sb("swq", [P, 4], FP32)
        swp = sb("swp", [P, 4], FP32)
        swp_row = sb("swp_row", [P, D], FP32)
        bp_row = sb("bp_row", [P, D], FP32)
        bv_row = sb("bv_row", [P, D], FP32)
        bq_col = sb("bq_col", [P, 4], FP32)
        bk_col = sb("bk_col", [P, 4], FP32)
        tanhs = sb("tanhs", [P, 2], FP32)
        xin = sb("xin", [P, TT, D], FP32)
        work = sb("work", [P, TT, D], FP32)
        q_int = sb("q_int", [P, TT, D], BF16)
        qT_int = sb("qT_int", [P, DC, N], BF16)
        stats = sb("stats", [P, TT, 6], FP32)
        mv = sb("mv", [P, TT, 2], FP32)
        std = sb("std", [P, TT], FP32)
        rstd = sb("rstd", [P, TT], FP32)
        amax = sb("amax", [P, TT], FP32)
        sx = sb("sx", [P, TT], FP32)
        inv = sb("inv", [P, TT], FP32)
        so = sb("so", [P, TT], FP32)
        sx_row = sb("sx_row", [P, N], FP32)
        ctx_raw = sb("ctx_raw", [P, CT_SLOTS, D], FP32)
        ctx_hi_flat = sb("ctx_hi", [P, DC * M], FP16)
        ctx_hi = ctx_hi_flat[:, :].rearrange("p (c m) -> p c m", c=DC)
        ctx_lo_flat = sb("ctx_lo", [P, DC * M], FP16)
        ctx_lo = ctx_lo_flat[:, :].rearrange("p (c m) -> p c m", c=DC)
        v_sb = sb("v_sb", [P, KT, D], FP32)
        qf = sb("qf", [P, N], FP32)
        zero_rows = qf
        q_hi = sb("q_hi", [P, N], FP16)
        q_lo = sb("q_lo", [P, N], FP16)
        k_hi = sb("k_hi", [P, M], FP16)
        k_lo = sb("k_lo", [P, M], FP16)
        k_stack = sb("k_stack", [KSPLIT + 1, 2, GH, M], FP16)
        q_stack = sb("q_stack", [KSPLIT + 1, 2, GH, N], FP16)
        piece_max = sb("piece_max", [P, GH * TT, PIECES], FP32)
        row_max = sb("row_max", [P, GH * TT], FP32)
        max_row = sb("max_row", [GH * TT, P], FP16)
        probs = sb("probs", [P, 2, GH, N], FP32)
        oT_sb = sb("oT_sb", [P, N], FP32)
        sum_sb = sb("sum_sb", [P, N], FP32)
        gate_raw = sum_sb[0:E, :]
        rsum = sb("rsum", [P, TT, GH], FP32)
        hT, actT = probs[:, 0], probs[:, 1]
        sig, gsil = oT_sb, sum_sb
        onehot = v_sb[:, 8, :].rearrange("p (t k e) -> p t k e", t=TT, k=TOPK)
        picked = v_sb[:, 9, :].rearrange("p (t k e) -> p t k e", t=TT, k=TOPK)
        scores, biased, masked, cum = (v_sb[:, 10, i * TT * E:(i + 1) * TT * E].rearrange("p (t e) -> p t e", t=TT)
                                       for i in range(4))
        top8 = v_sb[:, 11, 0:TT * E].rearrange("p (t q e) -> p t q e", t=TT, q=EGROUPS)
        gsum = sb("gsum", [P, TT, 8], FP32)
        gtop = sb("gtop", [P, TT, 8], FP32)
        gidx = sb("gidx", [P, TT, 8], U32)
        gidxf = sb("gidxf", [P, TT, 2], FP32)
        geq = sb("geq", [P, TT, 2, EGROUPS], FP32)
        gmask = sb("gmask", [P, TT, EGROUPS], FP32)
        etop = sb("etop", [P, TT, 8], FP32)
        eidx = sb("eidx", [P, TT, 8], U32)
        eidxf = sb("eidxf", [P, TT, TOPK], FP32)
        chosen = sb("chosen", [P, TT, E], BF16)
        carry = sb("carry", [P, E], FP32)
        pos = sb("pos", [P, TT, TOPK], FP32)
        over = sb("over", [P, TT, TOPK], FP32)
        slotf = sb("slotf", [P, TT, TOPK], FP32)
        slot = sb("slot", [P, TT, TOPK], I32)
        wk = sb("wk", [P, TT, TOPK], FP32)
        wsum = sb("wsum", [P, TT], FP32)
        wrec = sb("wrec", [P, TT], FP32)
        payload = sb("payload", [P, TT, TOPK, 2], FP32)
        slot_init = sb("slot_init", [P, E, 2], FP32)
        payload_i = payload[:, :, :, :].bitcast(I32)
        token = sb("token", [P, TT, TOPK], FP32)
        def part(buf, first, count, pattern, **sizes):
            return buf[:, first:first + count, :].rearrange(pattern, **sizes)

        w_len = DC * F
        homes = [v_sb[:, i * 6:i * 6 + 6, :].rearrange("p a n -> p (a n)") for i in range(2)]
        homes += [c[:, 0:6 * w_len].bitcast(FP32) for c in (ctx_hi_flat, ctx_lo_flat)]
        e_w1 = [h[:, 0:w_len].rearrange("p (c f) -> p c f", c=DC) for h in homes]
        e_w3 = [h[:, w_len:2 * w_len].rearrange("p (c f) -> p c f", c=DC) for h in homes]
        e_w2 = [h[:, 2 * w_len:3 * w_len].rearrange("p (f d) -> p f d", f=FC) for h in homes]
        p_sb = probs[:, :, :, :].rearrange("p a b n -> p (a b) n")
        e_rows = [p_sb[:, 0, :], p_sb[:, 1, :], oT_sb[:, :], sum_sb[:, :]]
        e_rowsT = part(p_sb, 2, 2, "p u (c n) -> p u c n", c=DC)
        e_y = [p_sb[:, 4 + u, :] for u in range(2)]
        e_act = p_sb[:, 6, :].rearrange("p (u f n) -> p u f n", u=2, f=FC)
        e_sig, e_gsil = p_sb[:, 7, 0:FC * P], p_sb[:, 7, FC * P:2 * FC * P]
        e_slots = [sb(f"e_slots{u}", [P, 2], FP32) for u in range(UN)]

        s_ps = [ctx.enter_context(nc.psum_tensor(f"s_ps{j}", [P, 512], FP32)) for j in range(GH)]
        r_ps = [ctx.enter_context(nc.psum_tensor(f"r_ps{i}", [P, 512], FP32)) for i in range(2)]
        o_ps = ctx.enter_context(nc.psum_tensor("o_ps", [P, 512], FP32))
        sum_ps = ctx.enter_context(nc.psum_tensor("sum_ps", [P, 512], FP32))

        consts_ready = sem("consts_ready")
        small_in = sem("small_in")
        raw_w_in = [sem(f"raw_w_in{i}") for i in range(2)]
        shared_in = sem("shared_in")
        w_int_ready = sem("w_int_ready")
        rows_init = sem("rows_init")
        row_consts_ready = sem("row_consts_ready")
        bank_full = [sem(f"bank_full{i}") for i in range(2)]
        bank_free = [sem(f"bank_free{i}") for i in range(2)]
        dve_step = sem("dve_step")
        act_step = sem("act_step")
        pool_step = sem("pool_step")
        dve_wait_carrier = sem("dve_wait_carrier")
        pool_wait_carrier = sem("pool_wait_carrier")
        tanh_ready = sem("tanh_ready")
        hi_ready = sem("hi_ready")
        x_in = sem("x_in")
        ctx_raw_in = [sem(f"ctx_raw_in{i}") for i in range(CT_SLOTS)]
        var_ready = sem("var_ready")
        std_ready = sem("std_ready")
        q_int_ready = sem("q_int_ready")
        ctx_lo_ready = sem("ctx_lo_ready")
        v_ready = sem("v_ready")
        x_biased = sem("x_biased")
        q_split = sem("q_split")
        k_split = sem("k_split")
        stack_in = sem("stack_in")
        row_max_ready = sem("row_max_ready")
        max_row_ready = sem("max_row_ready")
        max_out = sem("max_out")
        max_in = sem("max_in")
        scores_ready = sem("scores_ready")
        probs_ready = sem("probs_ready")
        probs_used = sem("probs_used")
        heads_copied = sem("heads_copied")
        rsum_ready = sem("rsum_ready")
        o_scaled = sem("o_scaled")
        evac_act = sem("evac_act")
        h_ready = sem("h_ready")
        h_out = sem("h_out")
        late_v_ready = sem("late_v_ready")
        late_v_read = sem("late_v_read")
        scores_sig = sem("scores_sig")
        sig_ready = sem("sig_ready")
        chosen_ready = sem("chosen_ready")
        act_ready = sem("act_ready")
        out_ready = sem("out_ready")
        out_written = sem("out_written")
        route_ready = sem("route_ready")
        slots_written = sem("slots_written")
        payload_free = sem("payload_free")
        e_w_in = [sem(f"e_w_in{u}") for u in range(UN)]
        e_slots_in = [sem(f"e_slots_in{u}") for u in range(UN)]
        e_rows_in = [sem(f"e_rows_in{u}") for u in range(UN)]
        e_sig_ready = sem("e_sig_ready")
        e_act_ready = sem("e_act_ready")
        e_y_ready = sem("e_y_ready")
        rows_added = sem("rows_added")
        experts_done = sem("experts_done")

        block = ctx.enter_context(nc.Block())

        def full(eng, it, *key):
            k = ring.bank(*key)
            eng.wait_ge(bank_full[k], ring.done(it, *key))
            return r_ps[k]

        def free_of(*key):
            return bank_free[ring.bank(*key)]

        @block.sync
        def _(sp):
            w_v = {"wq": wq.rearrange("(r p) d -> p r d", p=P), "wp": wp.rearrange("(r p) d -> p r d", p=P),
                   "wk": wkv[0:D, :].rearrange("(r p) d -> p r d", p=P),
                   "wv": wkv[D:2 * D, :].rearrange("(r p) d -> p r d", p=P)}
            sp.dma_start(probs[:, 0], w_v["wq"]).then_inc(raw_w_in[0], DMA)
            sp.dma_start(probs[:, 1], w_v["wp"]).then_inc(raw_w_in[1], DMA)
            for dst, src in ((bq_col, bq), (bk_col, bkv[0:D])):
                sp.dma_start(dst[:, :], src.rearrange("(r p) -> p r", p=P), allow_slow_non_contiguous=True).then_inc(small_in, DMA)
            for dst, src in ((bp_row, bp), (bv_row, bkv[D:2 * D]), (gbias, gate_bias)):
                sp.dma_start(dst[:, :], src.rearrange("(o n) -> o n", o=1).to_broadcast([P, src.shape[0]])
                             ).then_inc(small_in, DMA)
            for i, g_ in enumerate((g_xattn, g_ffn)):
                sp.dma_start(tanhs[:, i:i + 1], g_.rearrange("(o n) -> o n", o=1).to_broadcast([P, 1])
                             ).then_inc(small_in, DMA)
            sp.dma_start(gate_raw[:, :], gate_w).then_inc(small_in, DMA)
            sp.wait_ge(w_int_ready, 1)
            sp.dma_start(probs[:, 0], w_v["wk"]).then_inc(raw_w_in[0], DMA)
            sp.wait_ge(w_int_ready, 2)
            sp.dma_start(probs[:, 1], w_v["wv"]).then_inc(raw_w_in[1], DMA)
            sp.dma_start(sg[:, :, :], shared_gate.rearrange("(c p) n -> p c n", p=P)).then_inc(shared_in, DMA)
            sp.dma_start(su[:, :, :], shared_up.rearrange("(c p) n -> p c n", p=P)).then_inc(shared_in, DMA)
            sp.dma_start(sd[:, :, :], shared_down.rearrange("(c p) n -> p c n", p=P)).then_inc(shared_in, DMA)
            sp.wait_ge(consts_ready, 1)
            sp.dma_start(out[TOK:TOK + CAP, :], zero_rows[:, :]).then_inc(rows_init, DMA)
            sp.dma_start(h_scr[TOK:TOK + CAP, :], zero_rows[:, :]).then_inc(rows_init, DMA)
            sp.dma_start(slot_v.rearrange("e c w -> c e w"), slot_init[:, :, :]).then_inc(rows_init, DMA)
            with sp.Fori(0, B) as b:
                for t in range(KT):
                    if t == CT_SLOTS:
                        sp.wait_ge(h_out, b * DMA + DMA)
                        sp.wait_ge(out_written, b * DMA + DMA)
                        sp.dma_start(xin[:, :, :], x_v[b]).then_inc(x_in, DMA)
                    if t >= CT_SLOTS:
                        key = ("batch", "ctxT", t - CT_SLOTS)
                        sp.wait_ge(bank_full[ring.bank(*key)], ring.done(b, *key))
                    sp.dma_start(ctx_raw[0:rows(t), t % CT_SLOTS, :],
                                 ctx_in.rearrange("b m d -> b m d")[b, t * P:t * P + rows(t), :]
                                 ).then_inc(ctx_raw_in[t % CT_SLOTS], DMA)
                def stack_queries(g, r):
                    sp.wait_ge(q_split, b * GROUPS + g + 1)
                    for j in range(GH):
                        src = slice(j * DH, (j + 1) * DH)
                        for k, part in enumerate((q_hi, q_hi, q_lo)):
                            sp.dma_start(q_stack[k * DH:(k + 1) * DH, r, j, :], part[src, :]).then_inc(stack_in, DMA)

                def stack_keys(g, r):
                    sp.wait_ge(k_split, b * GROUPS + g + 1)
                    for j in range(GH):
                        src = slice(j * DH, (j + 1) * DH)
                        for k, part in enumerate((k_hi, k_lo, k_hi)):
                            sp.dma_start(k_stack[k * DH:(k + 1) * DH, r, j, :], part[src, :]).then_inc(stack_in, DMA)

                for g in range(GROUPS):
                    r = g % 2
                    if g == 0:
                        stack_keys(g, r)
                        stack_queries(g, r)
                    else:
                        stack_queries(g, r)
                        stack_keys(g, r)
                    sp.wait_ge(max_row_ready, b * GROUPS + g + 1)
                    sp.dma_start(max_scr[r], max_row[:, :]).then_inc(max_out, DMA)
                    sp.wait_ge(max_out, b * GROUPS * DMA + (g + 1) * DMA)
                    sp.dma_start(q_stack[KSPLIT:KSPLIT + 1, r, :, :].rearrange("o j n -> o (j n)"),
                                 max_scr[r].rearrange("(o a) n -> o (a n)", o=1)).then_inc(max_in, DMA)
                sp.wait_ge(h_ready, b + 1)
                sp.dma_start(h_v[b], work[:, :, :]).then_inc(h_out, DMA)
            sp.wait_ge(rows_init, 3 * DMA)
            with sp.Fori(0, E // UN) as it:
                for u in range(UN):
                    e = it * UN + u
                    key = ("expert", "ey", u)
                    sp.wait_ge(bank_full[ring.bank(*key)], it * ring.per["expert"] + ring.done(0, *key) - ring.per["expert"])
                    sp.dma_start(e_w1[u], w1_v[e]).then_inc(e_w_in[u], DMA)
                    sp.dma_start(e_w3[u], w3_v[e]).then_inc(e_w_in[u], DMA)
                    sp.dma_start(e_w2[u], w2_v[e]).then_inc(e_w_in[u], DMA)
                    sp.wait_ge(slots_written, B * TT * TOPK * DMA)
                    sp.wait_ge(experts_done, it * UN + u + 1)
                    sp.dma_start(e_slots[u][:, :], slot_v[e]).then_inc(e_slots_in[u], DMA)

        @block.tensor
        def _(pe):
            def open_tile(it, *key):
                k = ring.bank(*key)
                pe.wait_ge(bank_free[k], ring.done(it, *key))
                return r_ps[k]

            def close(last, *key):
                last.then_inc(bank_full[ring.bank(*key)], 1)

            pe.wait_ge(consts_ready, 1)
            for w, name in enumerate(("wqT", "wpT")):
                pe.wait_ge(w_int_ready, w + 1)
                for c in range(DC):
                    ps = open_tile(0, "setup", name, c)[:, :].bitcast(BF16)
                    for r in range(4):
                        last = nc.tensor.transpose(ps[:, r * P:(r + 1) * P], q_int[:, r, c * P:(c + 1) * P], identb[:, :])
                    close(last, "setup", name, c)
            for w, name in enumerate(("wkT", "wvT")):
                pe.wait_ge(raw_w_in[w], 2 * DMA)
                for c in range(DC):
                    ps = open_tile(0, "setup", name, c)
                    for r in range(4):
                        last = nc.tensor.transpose(ps[:, r * P:(r + 1) * P], probs[:, w, r, c * P:(c + 1) * P], ident[:, :])
                    close(last, "setup", name, c)
            pe.wait_ge(small_in, 8 * DMA)
            ps = open_tile(0, "setup", "gateT")
            for c in range(DC):
                last = nc.tensor.transpose(ps[:, c * E:(c + 1) * E], gate_raw[:, c * P:(c + 1) * P], ident[0:E, 0:E])
            close(last, "setup", "gateT")
            ps = open_tile(0, "setup", "swp")
            for r in range(4):
                last = nc.tensor.matmul(ps[:, r * P:(r + 1) * P], swp[:, r:r + 1].to_broadcast([P, P]), ident[:, :],
                                        start=True, stop=True)
            close(last, "setup", "swp")
            pe.wait_ge(shared_in, 3 * DMA)

            with pe.Fori(0, B) as b:
                def int_transposes(name):
                    for c in range(DC):
                        ps = open_tile(b, "batch", name, c)[:, :].bitcast(BF16)
                        for t in range(TT):
                            last = nc.tensor.transpose(ps[:, t * P:(t + 1) * P], q_int[:, t, c * P:(c + 1) * P], identb[:, :])
                        close(last, "batch", name, c)

                def values(t):
                    pe.wait_ge(ctx_lo_ready, b * KT + t + 1)
                    w = rows(t)
                    ps = open_tile(b, "batch", "v", t)
                    n = 0
                    for a, wt in ((ctx_hi, wkv_hi), (ctx_lo, wkv_hi), (ctx_hi, wkv_lo)):
                        for c in range(DC):
                            last = nc.tensor.matmul(ps[0:w, :], a[:, c, t * P:t * P + w], wt[:, 1, c, :],
                                                    start=(n == 0), stop=(n == 3 * DC - 1))
                            n += 1
                    close(last, "batch", "v", t)

                def late_value(i, n):
                    t = KT - V_LATE + i
                    a, wt = ((ctx_hi, wkv_hi), (ctx_lo, wkv_hi), (ctx_hi, wkv_lo))[n // DC]
                    w, c = rows(t), n % DC
                    last = nc.tensor.matmul(s_ps[i][0:w, :], a[:, c, t * P:t * P + w], wt[:, 1, c, :],
                                            start=(n == 0), stop=(n == 3 * DC - 1))
                    if n == 3 * DC - 1:
                        last.then_inc(late_v_ready, 1)

                def prep(key):
                    kind, g = key[0], key[1]
                    if kind == "v":
                        values(key[1])
                        return
                    r = g % 2
                    ps = open_tile(b, "batch", *key)
                    if kind == "q":
                        for c in range(DC):
                            last = nc.tensor.matmul(ps[:, :], wqT[:, c, g * P:(g + 1) * P], qT_int[:, c, :],
                                                    start=(c == 0), stop=(c == DC - 1))
                    elif kind == "k":
                        at, w = PIECE_AT[key[2]], PIECE[key[2]]
                        n = 0
                        for a, wt in ((ctx_hi, wkv_hi), (ctx_lo, wkv_hi), (ctx_hi, wkv_lo)):
                            for c in range(DC):
                                last = nc.tensor.matmul(ps[:, 0:w], wt[:, 0, c, g * P:(g + 1) * P], a[:, c, at:at + w],
                                                        start=(n == 0), stop=(n == 3 * DC - 1))
                                n += 1
                    elif kind == "max":
                        j, qt, i = key[2:]
                        if (j, qt, i) == (0, 0, 0):
                            pe.wait_ge(stack_in, b * GROUPS * 24 * DMA + (g + 1) * 24 * DMA)
                        at, w = PIECE_AT[i], PIECE[i]
                        last = nc.tensor.matmul(ps[:, 0:w], q_stack[0:KSPLIT, r, j, qt * P:(qt + 1) * P],
                                                k_stack[0:KSPLIT, r, j, at:at + w], start=True, stop=True)
                    else:
                        pe.wait_ge(row_max_ready, b * GROUPS + g + 1)
                        last = nc.tensor.transpose(ps[0:GH * TT, 0:P], row_max[:, :], ident[:, :])
                    close(last, "batch", *key)

                def scores_of(g, kt, j):
                    w = rows(kt)
                    if kt == 0 and j == 0:
                        pe.wait_ge(max_in, b * GROUPS * DMA + (g + 1) * DMA)
                    pe.wait_ge(probs_ready, b * GROUPS * KT * GH + (g * KT + kt) * GH + j + 1)
                    nc.tensor.matmul(s_ps[j][0:w, :], k_stack[:, g % 2, j, kt * P:kt * P + w],
                                     q_stack[:, g % 2, j, :], start=True, stop=True).then_inc(scores_ready, 1)

                def weighted(g, kt, is_v):
                    w = rows(kt)
                    if kt == 0:
                        pe.wait_ge(heads_copied, b * GROUPS + g + 1)
                    pe.wait_ge(probs_ready, b * GROUPS * KT * GH + (g * KT + kt + 1) * GH + GH)
                    half = (g * KT + kt) % 2
                    dst = o_ps if is_v else sum_ps
                    for j in range(GH):
                        h = g * GH + j
                        lhs = v_sb[0:w, kt, h * DH:(h + 1) * DH] if is_v else ones[0:w, :]
                        last = nc.tensor.matmul(dst[j * DH:(j + 1) * DH, :], lhs, probs[0:w, half, j, :],
                                                start=(kt == 0), stop=(kt == KT - 1))
                    if not is_v:
                        last.then_inc(probs_used, 1)

                def heads_out(g):
                    pe.wait_ge(heads_copied, b * GROUPS + g + 2)
                    ps = open_tile(b, "batch", "oT", g)
                    for t in range(TT):
                        last = nc.tensor.transpose(ps[:, t * P:(t + 1) * P], oT_sb[:, t * P:(t + 1) * P], ident[:, :])
                    close(last, "batch", "oT", g)
                    ps = open_tile(b, "batch", "sumT", g)
                    for t in range(TT):
                        last = nc.tensor.matmul(ps[:, t * GH:(t + 1) * GH], sum_sb[:, t * P:(t + 1) * P],
                                                ident[:, ::DH], start=True, stop=True)
                    close(last, "batch", "sumT", g)

                for t in range(KT):
                    uses = -(-(KT - t % CT_SLOTS) // CT_SLOTS)
                    pe.wait_ge(ctx_raw_in[t % CT_SLOTS], b * uses * DMA + (t // CT_SLOTS + 1) * DMA)
                    w = rows(t)
                    ps = open_tile(b, "batch", "ctxT", t)
                    for c in range(DC):
                        last = nc.tensor.transpose(ps[:, c * P:c * P + w], ctx_raw[0:w, t % CT_SLOTS, c * P:(c + 1) * P],
                                                   ident[0:w, 0:w])
                    close(last, "batch", "ctxT", t)
                    if values_after(t) is not None:
                        values(values_after(t))
                pe.wait_ge(ctx_lo_ready, b * KT + KT)
                for key in first_keys():
                    prep(key)
                pe.wait_ge(q_int_ready, b * 2 + 1)
                int_transposes("xT")
                ps = open_tile(b, "batch", "sx")
                for t in range(TT):
                    last = nc.tensor.matmul(ps[:, t * P:(t + 1) * P], sx[:, t:t + 1].to_broadcast([P, P]), ident[:, :],
                                            start=True, stop=True)
                close(last, "batch", "sx")
                pe.wait_ge(evac_act, b * (2 * DC + 1) + DC + 1)
                late = 0
                for key in first_queries():
                    prep(key)
                    if key[0] == "max" and late < V_LATE * 3 * DC:
                        late_value(late // (3 * DC), late % (3 * DC))
                        late += 1
                pe.wait_ge(late_v_read, b * V_LATE + V_LATE)
                for g in range(GROUPS):
                    for kt in range(KT):
                        tiles = prep_tiles(g + 1, kt) if g + 1 < GROUPS else []
                        for j in range(GH):
                            scores_of(g, kt, j)
                            for key in tiles[j:j + 1]:
                                prep(key)
                        tiles = tiles[GH:]
                        half = len(tiles) // 2
                        if kt:
                            weighted(g, kt - 1, True)
                        for key in tiles[:half]:
                            prep(key)
                        if kt:
                            weighted(g, kt - 1, False)
                        for key in tiles[half:]:
                            prep(key)
                        if kt == 1 and g:
                            heads_out(g - 1)
                    weighted(g, KT - 1, True)
                    weighted(g, KT - 1, False)
                heads_out(GROUPS - 1)
                pe.wait_ge(q_int_ready, b * 2 + 2)
                int_transposes("oiT")
                pe.wait_ge(evac_act, b * (2 * DC + 1) + 2 * DC + 1)
                for t in range(TT):
                    ps = open_tile(b, "batch", "y", t)
                    for c in range(DC):
                        last = nc.tensor.matmul(ps[:, :], qT_int[:, c, t * P:(t + 1) * P], wpT[:, c, :],
                                                start=(c == 0), stop=(c == DC - 1))
                    close(last, "batch", "y", t)
                pe.wait_ge(h_ready, b + 1)
                for c in range(DC):
                    ps = open_tile(b, "batch", "hT", c)
                    for t in range(TT):
                        last = nc.tensor.transpose(ps[:, t * P:(t + 1) * P], work[:, t, c * P:(c + 1) * P], ident[:, :])
                    close(last, "batch", "hT", c)
                for c in (DC - 2, DC - 1):
                    key = ("batch", "hT", c)
                    pe.wait_ge(free_of(*key), ring.done(b, *key) + 1)
                ps = open_tile(b, "batch", "logits")
                for t in range(TT):
                    for c in range(DC):
                        last = nc.tensor.matmul(ps[:, t * E:(t + 1) * E], hT[:, c, t * P:(t + 1) * P], gateT[:, c, :],
                                                start=(c == 0), stop=(c == DC - 1))
                close(last, "batch", "logits")
                for f in range(FSC):
                    for name, wt in (("gate", sg), ("up", su)):
                        ps = open_tile(b, "batch", name, f)
                        for c in range(DC):
                            last = nc.tensor.matmul(ps[:, :], wt[:, c, f * P:(f + 1) * P], hT[:, c, :],
                                                    start=(c == 0), stop=(c == DC - 1))
                        close(last, "batch", name, f)
                pe.wait_ge(chosen_ready, b + 1)
                ps = open_tile(b, "batch", "cum")
                for t in range(TT):
                    for u in range(t + 1):
                        last = nc.tensor.matmul(ps[:, t * E:(t + 1) * E], tri[:, :] if u == t else onesb[:, :],
                                                chosen[:, u, :], start=(u == 0), stop=(u == t))
                close(last, "batch", "cum")
                ps = open_tile(b, "batch", "total")
                for t in range(TT):
                    last = nc.tensor.matmul(ps[:, 0:E], onesb[:, :], chosen[:, t, :], start=(t == 0), stop=(t == TT - 1))
                close(last, "batch", "total")
                pe.wait_ge(act_ready, b * FSC + FSC)
                for t in range(TT):
                    ps = open_tile(b, "batch", "down", t)
                    for f in range(FSC):
                        last = nc.tensor.matmul(ps[:, :], actT[:, f, t * P:(t + 1) * P], sd[:, f, :],
                                                start=(f == 0), stop=(f == FSC - 1))
                    close(last, "batch", "down", t)
                if ("batch", "even") in ring.n:
                    ps = open_tile(b, "batch", "even")
                    close(nc.tensor.matmul(ps[0:DH, 0:DH], ones[:, :], ones[:, :], start=True, stop=True), "batch", "even")
            with pe.Fori(0, E // UN) as it:
                def rows_transposed(u):
                    pe.wait_ge(e_rows_in[u], it * DMA + DMA)
                    ps = open_tile(it, "expert", "hgT", u)
                    for c in range(DC):
                        last = nc.tensor.transpose(ps[:, c * P:(c + 1) * P], e_rows[u][:, c * P:(c + 1) * P], ident[:, :])
                    close(last, "expert", "hgT", u)

                rows_transposed(0)
                for u in range(UN):
                    pe.wait_ge(e_w_in[u], it * 3 * DMA + 3 * DMA)
                    pe.wait_ge(free_of("expert", "hgT", u), ring.done(it, "expert", "hgT", u) + 1)
                    for name, wt in (("eg", e_w1), ("eu", e_w3)):
                        ps = open_tile(it, "expert", name, u)
                        for f in range(FC):
                            for c in range(DC):
                                last = nc.tensor.matmul(ps[:, f * P:(f + 1) * P], wt[u][:, c, f * P:(f + 1) * P],
                                                        e_rowsT[:, u % 2, c, :], start=(c == 0), stop=(c == DC - 1))
                        close(last, "expert", name, u)
                    if u + 1 < UN:
                        rows_transposed(u + 1)
                    pe.wait_ge(e_act_ready, it * UN + u + 1)
                    ps = open_tile(it, "expert", "ey", u)
                    for f in range(FC):
                        last = nc.tensor.matmul(ps[:, :], e_act[:, u % 2, f, :], e_w2[u][:, f, :],
                                                start=(f == 0), stop=(f == FC - 1))
                    close(last, "expert", "ey", u)

        @block.scalar
        def _(act):
            step = Steps(act, act_step)
            act.wait_ge(small_in, 8 * DMA)
            nc.scalar.activation(tanhs[:, :], tanhs[:, :], ACT.Tanh).then_inc(tanh_ready, 1)
            for w, name in enumerate(("wqT", "wpT")):
                dst = (wqT, wpT)[w]
                for c in range(DC):
                    ps = full(act, 0, "setup", name, c)[:, :].bitcast(BF16)
                    nc.scalar.copy(dst[:, c, :], ps[:, 0:D]).then_inc(free_of("setup", name, c), 1)
            for w, name in enumerate(("wkT", "wvT")):
                for c in range(DC):
                    ps = full(act, 0, "setup", name, c)
                    nc.scalar.copy(wkv_hi[:, w, c, :], ps[:, :]).then_inc(hi_ready, 1)
            ps = full(act, 0, "setup", "gateT")
            nc.scalar.copy(gateT[:, :, :].rearrange("p c e -> p (c e)"), ps[:, 0:DC * E]).then_inc(free_of("setup", "gateT"), 1)
            act.sem_inc(probs_ready, GH)
            act.sem_inc(heads_copied, 1)
            hi_setup = 2 * DC
            hi_per = KT + GROUPS * PIECES

            with act.Fori(0, B) as b:
                step.enter(b, 8)

                def int_copies(name):
                    for c in range(DC):
                        ps = full(act, b, "batch", name, c)[:, :].bitcast(BF16)
                        nc.scalar.copy(qT_int[:, c, :], ps[:, 0:N]).then_inc(evac_act, 1)
                        act.wait_ge(evac_act, b * (2 * DC + 1) + (c + 1 if name == "xT" else DC + 1 + c + 1))
                        act.sem_inc(free_of("batch", name, c), 1)

                def prep(key):
                    kind, g = key[0], key[1]
                    if kind == "k":
                        at, w = PIECE_AT[key[2]], PIECE[key[2]]
                        if key[2] == 0 and (g > 0):
                            act.wait_ge(stack_in, b * GROUPS * 24 * DMA + g * 24 * DMA)
                        ps = full(act, b, "batch", *key)
                        nc.scalar.activation(k_hi[:, at:at + w], ps[:, 0:w], ACT.Identity,
                                             bias=bk_col[:, g:g + 1]).then_inc(hi_ready, 1)
                    elif kind == "maxT":
                        ps = full(act, b, "batch", *key)
                        nc.scalar.mul(max_row[:, :], ps[0:GH * TT, 0:P], -1.0).then_inc(max_row_ready, 1)
                        act.wait_ge(max_row_ready, b * GROUPS + g + 1)
                        act.sem_inc(free_of("batch", *key), 1)

                def exps(g, kt):
                    w = rows(kt)
                    half = (g * KT + kt) % 2
                    act.wait_ge(probs_used, b * GROUPS * KT + g * KT + kt + 1)
                    for j in range(GH):
                        act.wait_ge(scores_ready, b * GROUPS * KT * GH + (g * KT + kt) * GH + j + 1)
                        nc.scalar.activation(probs[0:w, half, j, :], s_ps[j][0:w, :], ACT.Exp).then_inc(probs_ready, 1)

                def copy_heads(g):
                    act.wait_ge(probs_used, b * GROUPS * KT + (g + 1) * KT + 2)
                    step.mark(nc.scalar.copy(oT_sb[:, :], o_ps[:, :]))
                    nc.scalar.copy(sum_sb[:, :], sum_ps[:, :]).then_inc(heads_copied, 1)

                for t in range(KT):
                    w = rows(t)
                    ps = full(act, b, "batch", "ctxT", t)
                    nc.scalar.copy(ctx_hi[:, :, t * P:t * P + w],
                                   ps[:, :].rearrange("p (c m) -> p c m", c=DC)[:, :, 0:w]).then_inc(hi_ready, 1)
                    if t == VAR_AT:
                        act.wait_ge(var_ready, b * 2 + 1)
                        nc.scalar.activation(std[:, :], mv[:, :, 1], ACT.Sqrt, bias=eps[:, :]).then_inc(std_ready, 1)
                for key in first_keys():
                    prep(key)
                int_copies("xT")
                ps = full(act, b, "batch", "sx")
                nc.scalar.copy(sx_row[:, :], ps[:, :]).then_inc(evac_act, 1)
                act.wait_ge(evac_act, b * (2 * DC + 1) + DC + 1)
                act.sem_inc(free_of("batch", "sx"), 1)
                for key in first_queries():
                    prep(key)
                for g in range(GROUPS):
                    for kt in range(KT):
                        exps(g, kt)
                        if g + 1 < GROUPS:
                            for key in prep_tiles(g + 1, kt):
                                prep(key)
                    copy_heads(g)
                int_copies("oiT")
                act.wait_ge(var_ready, b * 2 + 2)
                nc.scalar.activation(std[:, :], mv[:, :, 1], ACT.Sqrt, bias=eps[:, :]).then_inc(std_ready, 1)
                for c in range(DC):
                    ps = full(act, b, "batch", "hT", c)
                    nc.scalar.copy(hT[:, c, :], ps[:, :]).then_inc(free_of("batch", "hT", c), 1)
                ps = full(act, b, "batch", "logits")
                nc.scalar.activation(scores[:, :, :].rearrange("p t e -> p (t e)"), ps[:, 0:TT * E],
                                     ACT.Sigmoid).then_inc(scores_sig, 1)
                act.wait_ge(scores_sig, b + 1)
                act.sem_inc(free_of("batch", "logits"), 1)
                for f in range(FSC):
                    ps = full(act, b, "batch", "gate", f)
                    if f:
                        act.wait_ge(act_ready, b * FSC + f)
                    nc.scalar.activation(sig[:, :], ps[:, :], ACT.Sigmoid).then_inc(sig_ready, 1)
                act.wait_ge(out_ready, b + 1)
                nc.scalar.dma_start(out_v[b], xin[:, :, :]).then_inc(out_written, DMA)
                step.leave(B)
            with act.Fori(0, E // UN) as it:
                def copy_rows(u):
                    ps = full(act, it, "expert", "hgT", u)
                    nc.scalar.copy(e_rowsT[:, u % 2, :, :].rearrange("p c n -> p (c n)"), ps[:, :]
                                   ).then_inc(free_of("expert", "hgT", u), 1)

                copy_rows(0)
                for u in range(UN):
                    ps = full(act, it, "expert", "eg", u)
                    nc.scalar.activation(e_sig[:, :], ps[:, 0:FC * P], ACT.Sigmoid).then_inc(e_sig_ready, 1)
                    if u + 1 < UN:
                        copy_rows(u + 1)

        @block.vector
        def _(dve):
            step = Steps(dve, dve_step, dve_wait_carrier)
            V = nc.vector

            def row_scales(src, scale_out):
                step.mark(V.tensor_reduce(out=amax[:, :], in_=src[:, :, :], op=ALU.max, axis=X_AXIS, apply_absolute_value=True))
                step.settle()
                step.mark(V.tensor_scalar(scale_out[:, :], amax[:, :], 1.0 / 127.0, 1e-8, ALU.mult, ALU.max))
                step.settle()
                step.mark(V.reciprocal(inv[:, :], scale_out[:, :]))
                step.settle()

            def quantise_rows(src, tiles):
                for t in tiles:
                    step.mark(V.tensor_scalar(src[:, t, :], src[:, t, :], inv[:, t:t + 1], 127.0, ALU.mult, ALU.min))
                step.settle()
                for t in tiles:
                    step.mark(V.tensor_scalar(src[:, t, :], src[:, t, :], -127.0, ROUND, ALU.max, ALU.add))
                step.settle()
                for t in tiles:
                    last = V.tensor_scalar(q_int[:, t, :], src[:, t, :], ROUND, None, ALU.subtract)
                    if t < TT - 1:
                        step.mark(last)
                return last

            def quantise(src, scale_out):
                row_scales(src, scale_out)
                return quantise_rows(src, range(TT))

            dve.sem_inc(bank_free[0], 1)
            dve.sem_inc(bank_free[1], 1)
            dve.sem_inc(probs_used, 2)
            dve.sem_inc(h_out, DMA)
            dve.sem_inc(out_written, DMA)
            step.mark(V.memset(carry[:, :], 0.0))
            step.mark(V.memset(gsum[:, :, :], -3.0e38))
            step.mark(V.memset(k_stack[KSPLIT:KSPLIT + 1, :, :, :], 1.0))
            for w, scale in enumerate((swq, swp)):
                dve.wait_ge(raw_w_in[w], DMA)
                if w:
                    full(dve, 0, "setup", "wqT", DC - 1)
                    full(dve, 0, "setup", "wqT", DC - 2)
                quantise(probs[:, w], scale).then_inc(w_int_ready, 1)
            for w, name in enumerate(("wkT", "wvT")):
                for c in range(DC):
                    ps = full(dve, 0, "setup", name, c)
                    dve.wait_ge(hi_ready, w * DC + c + 1)
                    V.tensor_tensor(wkv_lo[:, w, c, :], ps[:, :], wkv_hi[:, w, c, :], ALU.subtract
                                    ).then_inc(free_of("setup", name, c), 1)
            dve.wait_ge(tanh_ready, 1)
            dve.wait_ge(rows_init, 3 * DMA)
            ps = full(dve, 0, "setup", "swp")
            V.tensor_scalar(swp_row[:, :], ps[:, :], tanhs[:, 0:1], None, ALU.mult).then_inc(free_of("setup", "swp"), 1)
            step.mark(V.tensor_scalar(bq_col[:, :], bq_col[:, :], SCALE, None, ALU.mult))
            V.tensor_scalar(bp_row[:, :], bp_row[:, :], tanhs[:, 0:1], None, ALU.mult).then_inc(row_consts_ready, 1)
            hi_setup, hi_per = 2 * DC, KT + GROUPS * PIECES

            with dve.Fori(0, B) as b:
                step.enter(b, 400)

                def variances():
                    for t in range(TT):
                        step.mark(V.bn_stats(stats[:, t, :], xin[:, t, :]))
                    step.settle()
                    step.carry_wait()
                    for t in range(TT):
                        last = V.bn_aggr(mv[:, t, :], stats[:, t, :])
                        if t < TT - 1:
                            step.mark(last)
                    last.then_inc(var_ready, 1)

                def inverse_std(n):
                    dve.wait_ge(std_ready, b * 2 + n)
                    step.mark(V.reciprocal(rstd[:, :], std[:, :]))
                    step.settle()

                def normalised(t):
                    return V.tensor_scalar(work[:, t, :], xin[:, t, :], mv[:, t, 0:1], rstd[:, t:t + 1],
                                           ALU.subtract, ALU.mult)

                def x_part(t):
                    if t == VAR_AT - 1:
                        dve.wait_ge(x_in, b * DMA + DMA)
                        variances()
                    elif t == VAR_AT + 1:
                        inverse_std(1)
                        for r in range(TT // 2):
                            step.mark(normalised(r))
                    elif t == VAR_AT + 2:
                        for r in range(TT // 2, TT):
                            step.mark(normalised(r))
                        step.settle()
                    elif t == VAR_AT + 3:
                        row_scales(work, sx)
                    elif VAR_AT + 4 <= t < VAR_AT + 4 + TT:
                        r = t - VAR_AT - 4
                        last = quantise_rows(work, [r])
                        if r == TT - 1:
                            last.then_inc(q_int_ready, 1)

                def prep(key):
                    kind, g = key[0], key[1]
                    if kind == "v":
                        value_tile(key[1])
                        return
                    if kind == "q":
                        if g:
                            dve.wait_ge(stack_in, b * GROUPS * 24 * DMA + g * 24 * DMA)
                        ps = full(dve, b, "batch", *key)
                        V.scalar_tensor_tensor(out=qf[:, :], in0=ps[:, :], scalar=swq[:, g:g + 1], in1=sx_row[:, :],
                                               op0=ALU.mult, op1=ALU.mult).then_inc(free_of("batch", *key), 1)
                        dve.wait_ge(free_of("batch", *key), ring.done(b, "batch", *key) + 1)
                        step.mark(V.tensor_scalar(qf[:, :], qf[:, :], SCALE, bq_col[:, g:g + 1], ALU.mult, ALU.add))
                        step.settle()
                        step.mark(V.tensor_copy(q_hi[:, :], qf[:, :]))
                        step.settle()
                        V.tensor_tensor(q_lo[:, :], qf[:, :], q_hi[:, :], ALU.subtract).then_inc(q_split, 1)
                    elif kind == "k":
                        i = key[2]
                        at, w = PIECE_AT[i], PIECE[i]
                        dve.wait_ge(hi_ready, b * hi_per + hi_setup + KT + g * PIECES + i + 1)
                        k = ring.bank("batch", *key)
                        V.scalar_tensor_tensor(out=k_lo[:, at:at + w], in0=r_ps[k][:, 0:w], scalar=bk_col[:, g:g + 1],
                                               in1=k_hi[:, at:at + w], op0=ALU.add, op1=ALU.subtract
                                               ).then_inc(free_of("batch", *key), 1)
                        if i == PIECES - 1:
                            dve.wait_ge(free_of("batch", *key), ring.done(b, "batch", *key) + 1)
                            dve.sem_inc(k_split, 1)
                    elif kind == "max":
                        j, qt, i = key[2:]
                        ps = full(dve, b, "batch", *key)
                        V.reduce_max(piece_max[:, j * TT + qt, i:i + 1], ps[:, 0:PIECE[i]], X_AXIS
                                     ).then_inc(free_of("batch", *key), 1)
                        if (j, qt, i) == (GH - 1, TT - 1, PIECES - 1):
                            dve.wait_ge(free_of("batch", *key), ring.done(b, "batch", *key) + 1)
                            V.reduce_max(row_max[:, :], piece_max[:, :, :], X_AXIS).then_inc(row_max_ready, 1)

                def heads_out(g):
                    po = full(dve, b, "batch", "oT", g)
                    pss = full(dve, b, "batch", "sumT", g)
                    V.reciprocal(rsum[:, :, :].rearrange("p t j -> p (t j)"), pss[:, 0:TT * GH]
                                 ).then_inc(free_of("batch", "sumT", g), 1)
                    dve.wait_ge(free_of("batch", "sumT", g), ring.done(b, "batch", "sumT", g) + 1)
                    for t in range(TT):
                        last = V.tensor_tensor(
                            work[:, t, g * P:(g + 1) * P].rearrange("p (j d) -> p j d", j=GH),
                            po[:, t * P:(t + 1) * P].rearrange("p (j d) -> p j d", j=GH),
                            rsum[:, t, :].unsqueeze(2).to_broadcast([P, GH, DH]), ALU.mult)
                        if t < TT - 1:
                            step.mark(last)
                    last.then_inc(free_of("batch", "oT", g), 1)
                    dve.wait_ge(free_of("batch", "oT", g), ring.done(b, "batch", "oT", g) + 1)

                def value_tile(t):
                    w = rows(t)
                    ps = full(dve, b, "batch", "v", t)
                    V.tensor_tensor(v_sb[0:w, t, :], ps[0:w, :], bv_row[0:w, :], ALU.add).then_inc(free_of("batch", "v", t), 1)

                for t in range(KT):
                    w = rows(t)
                    dve.wait_ge(hi_ready, b * hi_per + hi_setup + t + 1)
                    ps = r_ps[ring.bank("batch", "ctxT", t)]
                    V.tensor_tensor(ctx_lo[:, :, t * P:t * P + w],
                                    ps[:, :].rearrange("p (c m) -> p c m", c=DC)[:, :, 0:w],
                                    ctx_hi[:, :, t * P:t * P + w], ALU.subtract).then_inc(ctx_lo_ready, 1)
                    dve.wait_ge(ctx_lo_ready, b * KT + t + 1)
                    dve.sem_inc(free_of("batch", "ctxT", t), 1)
                    if values_after(t) is not None:
                        value_tile(values_after(t))
                    x_part(t)
                late = 0
                for key in first_keys() + first_queries():
                    prep(key)
                    if key[0] == "max":
                        late += 1
                        i = late // (3 * DC) - 1
                        if late % (3 * DC) == 2 and 0 <= i < V_LATE:
                            t = KT - V_LATE + i
                            dve.wait_ge(late_v_ready, b * V_LATE + i + 1)
                            V.tensor_tensor(v_sb[0:rows(t), t, :], s_ps[i][0:rows(t), :], bv_row[0:rows(t), :], ALU.add
                                            ).then_inc(late_v_read, 1)
                for g in range(GROUPS):
                    for kt in range(KT):
                        if g + 1 < GROUPS:
                            for key in prep_tiles(g + 1, kt):
                                prep(key)
                        if kt == 1 and g:
                            heads_out(g - 1)
                heads_out(GROUPS - 1)
                quantise(work, so).then_inc(q_int_ready, 1)
                dve.wait_ge(x_biased, b + 1)
                for t in range(TT):
                    ps = full(dve, b, "batch", "y", t)
                    V.scalar_tensor_tensor(out=work[:, t, :], in0=ps[:, :], scalar=so[:, t:t + 1], in1=swp_row[:, :],
                                           op0=ALU.mult, op1=ALU.mult).then_inc(free_of("batch", "y", t), 1)
                    dve.wait_ge(free_of("batch", "y", t), ring.done(b, "batch", "y", t) + 1)
                    step.mark(V.tensor_tensor(xin[:, t, :], xin[:, t, :], work[:, t, :], ALU.add))
                step.settle()
                variances()
                inverse_std(2)
                for t in range(TT):
                    last = normalised(t)
                    if t < TT - 1:
                        step.mark(last)
                last.then_inc(h_ready, 1)

                def scores_in_groups():
                    dve.wait_ge(scores_sig, b + 1)
                    step.mark(V.tensor_tensor(biased[:, :, :], scores[:, :, :],
                                              gbias[:, :].unsqueeze(1).to_broadcast([P, TT, E]), ALU.add))
                    step.settle()
                    step.carry_wait()
                    for t in range(TT):
                        for q in range(EGROUPS):
                            step.mark(V.max(top8[:, t, q, :], biased[:, t, q * EPG:(q + 1) * EPG]))
                    step.settle()
                    step.mark(V.tensor_tensor(gsum[:, :, 0:EGROUPS], top8[:, :, :, 0], top8[:, :, :, 1], ALU.add))
                    step.settle()
                    step.carry_wait()
                    for t in range(TT):
                        step.mark(V.max(gtop[:, t, :], gsum[:, t, :]))
                    step.settle()
                    step.carry_wait()
                    for t in range(TT):
                        step.mark(V.max_index(gidx[:, t, :], gtop[:, t, :], gsum[:, t, :]))
                    step.settle()

                def best_groups_and_experts():
                    step.mark(V.tensor_copy(gidxf[:, :, :], gidx[:, :, 0:2]))
                    step.settle()
                    for k in range(2):
                        step.mark(V.tensor_tensor(geq[:, :, k, :], lane[:, 0:EGROUPS].unsqueeze(1).to_broadcast([P, TT, EGROUPS]),
                                                  gidxf[:, :, k:k + 1].to_broadcast([P, TT, EGROUPS]), ALU.is_equal))
                    step.settle()
                    step.mark(V.tensor_tensor(gmask[:, :, :], geq[:, :, 0, :], geq[:, :, 1, :], ALU.add))
                    step.settle()
                    step.mark(V.tensor_tensor(masked[:, :, :].rearrange("p t (q e) -> p (t q) e", q=EGROUPS),
                                              biased[:, :, :].rearrange("p t (q e) -> p (t q) e", q=EGROUPS),
                                              gmask[:, :, :].rearrange("p t q -> p (t q)").unsqueeze(2).to_broadcast([P, TT * EGROUPS, EPG]),
                                              ALU.mult))
                    step.settle()
                    step.carry_wait()
                    for t in range(TT):
                        step.mark(V.max(etop[:, t, :], masked[:, t, :]))
                    step.settle()
                    step.carry_wait()
                    for t in range(TT):
                        step.mark(V.max_index(eidx[:, t, :], etop[:, t, :], masked[:, t, :]))
                    step.settle()

                def expert_masks():
                    step.mark(V.tensor_copy(eidxf[:, :, :], eidx[:, :, 0:TOPK]))
                    step.settle()
                    for t in range(TT):
                        step.mark(V.tensor_tensor(onehot[:, t, :, :], lane[:, :].unsqueeze(1).to_broadcast([P, TOPK, E]),
                                                  eidxf[:, t, :].unsqueeze(2).to_broadcast([P, TOPK, E]), ALU.is_equal))
                    step.settle()
                    with nc.allow_low_precision("counts of 0 and 1") if hasattr(nc, "allow_low_precision") else ExitStack():
                        V.tensor_reduce(out=chosen[:, :, :], in_=onehot[:, :, :, :].rearrange("p t k e -> p t e k"),
                                        op=ALU.add, axis=X_AXIS).then_inc(chosen_ready, 1)
                    for t in range(TT):
                        step.mark(V.tensor_tensor(picked[:, t, :, :], onehot[:, t, :, :],
                                                  scores[:, t, :].unsqueeze(1).to_broadcast([P, TOPK, E]), ALU.mult))
                    step.settle()

                def expert_weights():
                    step.mark(V.tensor_reduce(out=wk[:, :, :], in_=picked[:, :, :, :], op=ALU.add, axis=X_AXIS))
                    step.settle()
                    step.mark(V.tensor_reduce(out=wsum[:, :], in_=wk[:, :, :], op=ALU.add, axis=X_AXIS))
                    step.settle()
                    step.mark(V.tensor_scalar(wsum[:, :], wsum[:, :], 1e-20, None, ALU.add))
                    step.settle()
                    step.mark(V.reciprocal(wrec[:, :], wsum[:, :]))
                    step.settle()
                    dve.wait_ge(payload_free, b + 1)
                    for t in range(TT):
                        step.mark(V.tensor_scalar(payload[:, t, :, 1], wk[:, t, :], wrec[:, t:t + 1], 2.0, ALU.mult, ALU.mult))
                    step.settle()

                def swiglu(f):
                    dve.wait_ge(sig_ready, b * FSC + f + 1)
                    pg = r_ps[ring.bank("batch", "gate", f)]
                    V.tensor_tensor(gsil[:, :], pg[:, :], sig[:, :], ALU.mult).then_inc(free_of("batch", "gate", f), 1)
                    dve.wait_ge(free_of("batch", "gate", f), ring.done(b, "batch", "gate", f) + 1)
                    pu = full(dve, b, "batch", "up", f)
                    V.tensor_tensor(actT[:, f, :], pu[:, :], gsil[:, :], ALU.mult).then_inc(act_ready, 1)
                    dve.wait_ge(act_ready, b * FSC + f + 1)
                    dve.sem_inc(free_of("batch", "up", f), 1)

                for f, part in enumerate((scores_in_groups, best_groups_and_experts, expert_masks, expert_weights)):
                    swiglu(f)
                    part()
                ps = full(dve, b, "batch", "cum")
                V.tensor_tensor(cum[:, :, :], ps[:, 0:TT * E].rearrange("p (t e) -> p t e", t=TT),
                                carry[:, :].unsqueeze(1).to_broadcast([P, TT, E]), ALU.add).then_inc(free_of("batch", "cum"), 1)
                dve.wait_ge(free_of("batch", "cum"), ring.done(b, "batch", "cum") + 1)
                ps = full(dve, b, "batch", "total")
                V.tensor_tensor(carry[:, :], ps[:, 0:E], carry[:, :], ALU.add).then_inc(free_of("batch", "total"), 1)
                def add_shared(t):
                    ps = full(dve, b, "batch", "down", t)
                    V.scalar_tensor_tensor(out=xin[:, t, :], in0=ps[:, :], scalar=tanhs[:, 1:2], in1=xin[:, t, :],
                                           op0=ALU.mult, op1=ALU.add).then_inc(free_of("batch", "down", t), 1)

                for t in range(TT):
                    step.mark(V.tensor_tensor(picked[:, t, :, :], onehot[:, t, :, :],
                                              cum[:, t, :].unsqueeze(1).to_broadcast([P, TOPK, E]), ALU.mult))
                step.settle()
                add_shared(0)
                step.mark(V.tensor_reduce(out=pos[:, :, :], in_=picked[:, :, :, :], op=ALU.add, axis=X_AXIS))
                step.settle()
                add_shared(1)
                step.mark(V.tensor_scalar(over[:, :, :], pos[:, :, :], float(CAP), float(2 * E * CAP), ALU.is_ge, ALU.mult))
                step.mark(V.scalar_tensor_tensor(out=slotf[:, :, :], in0=eidxf[:, :, :], scalar=float(CAP), in1=pos[:, :, :],
                                                 op0=ALU.mult, op1=ALU.add))
                step.settle()
                V.tensor_tensor(slot[:, :, :], slotf[:, :, :], over[:, :, :], ALU.add).then_inc(route_ready, 1)
                for t in range(2, TT):
                    add_shared(t)
                dve.wait_ge(free_of("batch", "down", TT - 1), ring.done(b, "batch", "down", TT - 1) + 1)
                dve.sem_inc(out_ready, 1)
                if ("batch", "even") in ring.n:
                    full(dve, b, "batch", "even")
                    dve.sem_inc(free_of("batch", "even"), 1)
                step.leave(B)
            with dve.Fori(0, E // UN) as it:
                for u in range(UN):
                    dve.wait_ge(e_sig_ready, it * UN + u + 1)
                    pg = r_ps[ring.bank("expert", "eg", u)]
                    key = ("expert", "eg", u)
                    V.tensor_tensor(e_gsil[:, :], pg[:, 0:FC * P], e_sig[:, :], ALU.mult).then_inc(free_of(*key), 1)
                    dve.wait_ge(free_of(*key), ring.done(it, *key) + 1)
                    pu = full(dve, it, "expert", "eu", u)
                    V.tensor_tensor(e_act[:, u % 2, :, :].rearrange("p f n -> p (f n)"), pu[:, 0:FC * P], e_gsil[:, :], ALU.mult
                                    ).then_inc(e_act_ready, 1)
                    dve.wait_ge(e_act_ready, it * UN + u + 1)
                    dve.sem_inc(free_of("expert", "eu", u), 1)
                    dve.wait_ge(e_slots_in[u], it * DMA + DMA)
                    dve.wait_ge(experts_done, it * UN + u + UN - 1)
                    ps = full(dve, it, "expert", "ey", u)
                    V.tensor_scalar(e_y[u % 2][:, :], ps[:, :], e_slots[u][:, 1:2], tanhs[:, 1:2], ALU.mult, ALU.mult
                                    ).then_inc(e_y_ready, 1)
                    dve.wait_ge(e_y_ready, it * UN + u + 1)
                    dve.sem_inc(free_of("expert", "ey", u), 1)

        @block.gpsimd
        def _(pool):
            step = Steps(pool, pool_step, pool_wait_carrier)
            G = nc.gpsimd
            for m in (ident, identb):
                step.mark(G.memset(m[:, :], 0.0))
            for m, v in ((onesb, 1.0), (ones, 1.0), (tri, 1.0), (eps, EPS), (zero_rows, 0.0), (slot_init, 0.0)):
                ap = m[:, :, :] if m is slot_init else m[:, :]
                step.mark(G.memset(ap, v))
            step.mark(G.iota(lane[:, :], [[1, E]], base=0, channel_multiplier=0, allow_small_or_imprecise_dtypes=True))
            step.settle()
            for m in (ident, identb):
                step.mark(G.affine_select(out=m[:, :], in_=m[:, :], compare_op=ALU.not_equal, fill=1.0, base=0,
                                          pattern=[[-1, P]], channel_multiplier=1))
            step.mark(G.affine_select(out=tri[:, :], in_=tri[:, :], compare_op=ALU.is_gt, fill=0.0, base=0,
                                      pattern=[[1, P]], channel_multiplier=-1))
            step.mark(G.iota(slot_init[:, :, 0].bitcast(I32), [[0, E]], base=TOK, channel_multiplier=1))
            step.settle()
            pool.sem_inc(consts_ready, 1)
            pool.sem_inc(payload_free, 1)
            pool.sem_inc(experts_done, UN)
            step.mark(G.iota(token[:, :, :], [[P, TT], [0, TOPK]], base=0, channel_multiplier=1,
                             allow_small_or_imprecise_dtypes=True))
            pool.wait_ge(row_consts_ready, 1)
            pool.wait_ge(rows_init, 3 * DMA)
            with pool.Fori(0, B) as b:
                step.enter(b, 8)
                pool.wait_ge(q_int_ready, b * 2 + 1)
                for t in range(TT):
                    last = G.tensor_tensor(xin[:, t, :], xin[:, t, :], bp_row[:, :], ALU.add)
                    if t < TT - 1:
                        step.mark(last)
                last.then_inc(x_biased, 1)
                pool.wait_ge(payload_free, b + 1)
                step.settle()
                step.carry_wait()
                step.mark(G.tensor_copy(payload_i[:, :, :, 0], token[:, :, :]))
                step.settle()
                step.carry_wait()
                step.mark(G.tensor_scalar(token[:, :, :], token[:, :, :], float(N), None, ALU.add))
                pool.wait_ge(route_ready, b + 1)
                step.carry_wait()
                for t in range(TT):
                    for k in range(TOPK):
                        G.indirect_dma_start(out=slot_scr, out_offset=bass.IndirectOffsetOnAxis(ap=slot[:, t, k:k + 1], axis=0),
                                             in_=payload[:, t, k, :], in_offset=None, bounds_check=E * CAP - 1,
                                             oob_is_err=False).then_inc(slots_written, DMA)
                pool.wait_ge(slots_written, b * TT * TOPK * DMA + TT * TOPK * DMA)
                pool.sem_inc(payload_free, 1)
                step.leave(B)
            pool.wait_ge(h_out, B * DMA + DMA)
            pool.wait_ge(out_written, B * DMA + DMA)

            def gather(it, u):
                pool.wait_ge(e_slots_in[u], it * DMA + DMA)
                key = ("expert", "hgT", u)
                pool.wait_ge(bank_full[ring.bank(*key)], it * ring.per["expert"] + ring.done(0, *key) - ring.per["expert"])
                step.carry_wait()
                G.indirect_dma_start(out=e_rows[u][:, :], out_offset=None, in_=h_scr,
                                     in_offset=bass.IndirectOffsetOnAxis(ap=e_slots[u][:, 0:1].bitcast(I32), axis=0),
                                     bounds_check=TOK + CAP - 1, oob_is_err=True).then_inc(e_rows_in[u], DMA)

            def add_rows(it, u):
                pool.wait_ge(e_y_ready, it * UN + u + 1)
                step.carry_wait()
                G.indirect_dma_start(out=out, out_offset=bass.IndirectOffsetOnAxis(ap=e_slots[u][:, 0:1].bitcast(I32), axis=0),
                                     in_=e_y[u % 2][:, :], in_offset=None, bounds_check=TOK + CAP - 1, oob_is_err=True,
                                     compute_op=ALU.add).then_inc(rows_added, DMA)

            def finish(it, u):
                pool.wait_ge(rows_added, it * UN * DMA + (u + 1) * DMA)
                pool.sem_inc(experts_done, 1)

            gather(0, 0)
            gather(0, 1)
            with pool.Fori(0, E // UN - 1) as it:
                for u in range(UN):
                    add_rows(it, u)
                    gather(it + (u + 2) // UN, (u + 2) % UN)
                    finish(it, u)
            for u in range(UN):
                add_rows(E // UN - 1, u)
                if u + 2 < UN:
                    gather(E // UN - 1, u + 2)
                finish(E // UN - 1, u)


_INS = ["x", "ctx_2048", "g_xattn", "g_ffn", "L0_xattn_wq", "L0_xattn_bq", "L0_xattn_wkv", "L0_xattn_bkv",
        "L0_xattn_wp", "L0_xattn_bp", "L0_ffn_gate_w", "L0_ffn_gate_bias", "L0_ffn_w1", "L0_ffn_w2", "L0_ffn_w3",
        "L0_ffn_shared_gate", "L0_ffn_shared_up", "L0_ffn_shared_down"]


def kernel(**inputs):
    import numpy as np
    import concourse.bacc as bacc
    from concourse.bass_utils import run_bass_kernel_spmd

    nc = bacc.Bacc("TRN2", target_bir_lowering=False, num_devices=1)
    arrays, args = {}, []
    for name in _INS:
        a = np.ascontiguousarray(inputs[name])
        arrays[f"in_{name}"] = a
        args.append(nc.dram_tensor(f"in_{name}", a.shape, mybir.dt.from_np(a.dtype), kind="ExternalInput").ap())
    out = nc.dram_tensor("out_rows", (TOK + CAP, D), FP32, kind="ExternalOutput").ap()
    by = dict(zip(_INS, args))
    build(nc, by["x"], by["ctx_2048"], by["g_xattn"], by["g_ffn"], by["L0_xattn_wq"], by["L0_xattn_bq"],
          by["L0_xattn_wkv"], by["L0_xattn_bkv"], by["L0_xattn_wp"], by["L0_xattn_bp"], by["L0_ffn_gate_w"],
          by["L0_ffn_gate_bias"], by["L0_ffn_w1"], by["L0_ffn_w2"], by["L0_ffn_w3"], by["L0_ffn_shared_gate"],
          by["L0_ffn_shared_up"], by["L0_ffn_shared_down"], out)
    r = run_bass_kernel_spmd(nc, [arrays], core_ids=[0])
    return r.results[0]["out_rows"][0:TOK].reshape(B, N, D)
```
